# Optimizing a Trainium2 kernel written in Bass

```python
import numpy as np
import jax
import jax.numpy as jnp

def _softmax(x, axis=-1):
    return jax.nn.softmax(x, axis=axis)

def _gelu(x):
    return jax.nn.gelu(x, approximate=True)

def _silu(x):
    return jax.nn.silu(x)

def _sigmoid(x):
    return jax.nn.sigmoid(x)

def _layernorm(x, axis=-1, eps=1e-05):
    m = jnp.mean(x, axis=axis, keepdims=True)
    v = jnp.var(x, axis=axis, keepdims=True)
    return (x - m) / jnp.sqrt(v + eps)

def _scatter_add(tgt, idx, src, axis=0):
    return tgt.at[idx].add(src)

def _segment_sum(src, seg, n):
    return jax.ops.segment_sum(src, seg, n)
kernel_name = 'mk_adj_resnorm_d2_adj_r2_e32a69'

def setup_inputs(seed: int=0):
    np.random.seed(seed)
    _w = jnp.asarray

    def _rec_inputs():
        import jax
        import jax.numpy as jnp
        _gk = jax.random.key(seed)
        x = -1.394e-06 + 0.9999 * jax.random.normal(jax.random.fold_in(_gk, 1), (4096, 256), jnp.float32)
        _a = jax.random.bernoulli(jax.random.fold_in(_gk, 2), 0.00195312, (4096, 4096))
        _a = jnp.logical_or(_a, jnp.eye(4096, dtype=bool))
        adj = _a
        return (x, adj)
    x, adj = _rec_inputs()

    def _L0_gnn_setup():
        import jax, jax.numpy as jnp
        import numpy as np
        import math
        N = 4096
        D_IN = 256
        LOCAL_D = 256
        GLOBAL_D = 256
        key = jax.random.key(seed)
        ks = jax.random.split(key, 16)
        s = 1.0 / math.sqrt(D_IN)
        adj = jax.random.bernoulli(ks[0], 0.01, (N, N))
        adj = adj | jnp.eye(N, dtype=bool)
        return {'adj_matrix': adj, 'x': jax.random.normal(ks[1], (N, D_IN), jnp.float32), 'masked_x': jax.random.normal(ks[2], (N, D_IN), jnp.float32), 'Wlq': jax.random.normal(ks[3], (D_IN, LOCAL_D), jnp.float32) * s, 'Wlk': jax.random.normal(ks[4], (D_IN, LOCAL_D), jnp.float32) * s, 'Wlv': jax.random.normal(ks[5], (D_IN, D_IN), jnp.float32) * s, 'blv': jax.random.normal(ks[6], (D_IN,), jnp.float32) * 0.01, 'Wgq': jax.random.normal(ks[7], (D_IN, GLOBAL_D), jnp.float32) * s, 'Wgk': jax.random.normal(ks[8], (D_IN, GLOBAL_D), jnp.float32) * s, 'Wgv': jax.random.normal(ks[9], (D_IN, D_IN), jnp.float32) * s, 'bgv': jax.random.normal(ks[10], (D_IN,), jnp.float32) * 0.01, 'Wes': jax.random.normal(ks[11], (D_IN, 1), jnp.float32) * s, 'Wev': jax.random.normal(ks[12], (D_IN, D_IN), jnp.float32) * s, 'bev': jax.random.normal(ks[13], (D_IN,), jnp.float32) * 0.01}
    _L0_gnn_all = _L0_gnn_setup()
    _L0_gnn_in = {k: v for k, v in _L0_gnn_all.items() if k in ('masked_x', 'Wlq', 'Wlk', 'Wlv', 'blv', 'Wgq', 'Wgk', 'Wgv', 'bgv', 'Wes', 'Wev', 'bev')}
    del _L0_gnn_all

    def _L1_gnn_setup():
        import jax, jax.numpy as jnp
        import numpy as np
        N = 4096
        D = 256
        NEG = -1e+30
        key = jax.random.key(seed)
        ks = jax.random.split(key, 5)
        neuron_states = jax.random.normal(ks[0], (N, D), dtype=jnp.float32)
        adjacency = jax.random.bernoulli(ks[1], 0.05, (N, N))
        Wq = jax.random.normal(ks[2], (D, D), dtype=jnp.float32) / np.sqrt(D)
        Wk = jax.random.normal(ks[3], (D, D), dtype=jnp.float32) / np.sqrt(D)
        Wv = jax.random.normal(ks[4], (D, D), dtype=jnp.float32) / np.sqrt(D)
        return {'neuron_states': neuron_states, 'adjacency': adjacency, 'Wq': Wq, 'Wk': Wk, 'Wv': Wv}
    _L1_gnn_all = _L1_gnn_setup()
    _L1_gnn_in = {k: v for k, v in _L1_gnn_all.items() if k in ('Wq', 'Wk', 'Wv')}
    del _L1_gnn_all
    return {'x': x, 'adj': adj, 'L0_gnn_masked_x': _L0_gnn_in['masked_x'], 'L0_gnn_Wlq': _L0_gnn_in['Wlq'], 'L0_gnn_Wlk': _L0_gnn_in['Wlk'], 'L0_gnn_Wlv': _L0_gnn_in['Wlv'], 'L0_gnn_blv': _L0_gnn_in['blv'], 'L0_gnn_Wgq': _L0_gnn_in['Wgq'], 'L0_gnn_Wgk': _L0_gnn_in['Wgk'], 'L0_gnn_Wgv': _L0_gnn_in['Wgv'], 'L0_gnn_bgv': _L0_gnn_in['bgv'], 'L0_gnn_Wes': _L0_gnn_in['Wes'], 'L0_gnn_Wev': _L0_gnn_in['Wev'], 'L0_gnn_bev': _L0_gnn_in['bev'], 'L1_gnn_Wq': _L1_gnn_in['Wq'], 'L1_gnn_Wk': _L1_gnn_in['Wk'], 'L1_gnn_Wv': _L1_gnn_in['Wv']}

def reference(x, adj, L0_gnn_masked_x, L0_gnn_Wlq, L0_gnn_Wlk, L0_gnn_Wlv, L0_gnn_blv, L0_gnn_Wgq, L0_gnn_Wgk, L0_gnn_Wgv, L0_gnn_bgv, L0_gnn_Wes, L0_gnn_Wev, L0_gnn_bev, L1_gnn_Wq, L1_gnn_Wk, L1_gnn_Wv):
    import jax
    import jax.numpy as jnp

    def _L0_gnn_ref(adj_matrix, x, masked_x, Wlq, Wlk, Wlv, blv, Wgq, Wgk, Wgv, bgv, Wes, Wev, bev):
        import jax, jax.numpy as jnp
        import numpy as np
        import math
        N = 4096
        D_IN = 256
        LOCAL_D = 256
        GLOBAL_D = 256
        scale = 1.0 / math.sqrt(D_IN)
        x_bar = jnp.mean(x, axis=0, keepdims=True)
        lQ = masked_x @ Wlq
        lK = x @ Wlk
        lV = x @ Wlv + blv
        gQ = masked_x @ Wgq
        gK = x_bar @ Wgk
        gV = x_bar @ Wgv + bgv
        es = masked_x @ Wes
        eV = masked_x @ Wev + bev
        local_scores = lQ @ lK.T * scale
        local_scores = jnp.where(adj_matrix, local_scores, jnp.float32(-1000000000.0))
        global_scores = gQ @ gK.T * scale
        max_score = jnp.maximum(jnp.max(local_scores, axis=1, keepdims=True), jnp.maximum(global_scores, es))
        le = jnp.exp(local_scores - max_score)
        ge = jnp.exp(global_scores - max_score)
        ee = jnp.exp(es - max_score)
        denom = jnp.sum(le, axis=-1, keepdims=True) + ge + ee
        res = le / denom @ lV + ge / denom * gV + ee / denom * eV
        x_recon = jnp.maximum(res, masked_x)
        return x_recon

    def _L1_gnn_ref(neuron_states, adjacency, Wq, Wk, Wv):
        import jax, jax.numpy as jnp
        import numpy as np
        N = 4096
        D = 256
        NEG = -1e+30
        q = neuron_states @ Wq.T
        k = neuron_states @ Wk.T
        v = neuron_states @ Wv.T
        mask = adjacency.T
        scores = jnp.where(mask, q @ k.T, NEG)
        attn = jax.nn.softmax(scores, axis=1)
        attn = jnp.where(mask, attn, 0.0)
        return attn @ v
    x = _layernorm(x + _L0_gnn_ref(adj, x, L0_gnn_masked_x, L0_gnn_Wlq, L0_gnn_Wlk, L0_gnn_Wlv, L0_gnn_blv, L0_gnn_Wgq, L0_gnn_Wgk, L0_gnn_Wgv, L0_gnn_bgv, L0_gnn_Wes, L0_gnn_Wev, L0_gnn_bev), axis=-1)
    x = _layernorm(x + _L1_gnn_ref(x, adj, L1_gnn_Wq, L1_gnn_Wk, L1_gnn_Wv), axis=-1)
    return x

_drawn_inputs = setup_inputs


def setup_inputs(seed=0):
    import zlib

    import numpy as np

    out = dict(_drawn_inputs(seed))
    spreads = {}
    factors = {'L0_gnn_blv': 3.996,
     'L0_gnn_Wgq': 8.0,
     'L0_gnn_Wgk': 8.0,
     'L0_gnn_Wgv': 8.0,
     'L0_gnn_bgv': 26.053,
     'L0_gnn_bev': 25.018}
    for name, (base, spread) in spreads.items():
        noise = np.random.default_rng([zlib.crc32(name.encode()), seed]).standard_normal(out[name].shape)
        drawn = base * np.exp(spread * noise) if base else spread * noise
        out[name] = jnp.asarray(drawn.astype(out[name].dtype))
    for name, factor in factors.items():
        out[name] = (out[name] * factor).astype(out[name].dtype)
    return out
```

```python
from contextlib import ExitStack

import concourse.bass as bass
from concourse import mybir

F32 = mybir.dt.float32
F32R = mybir.dt.float32r
BF16 = mybir.dt.bfloat16
U8 = mybir.dt.uint8
U16 = mybir.dt.uint16
ALU = mybir.AluOpType
ACT = mybir.ActivationFunctionType
AX = mybir.AxisListType

P = 128
N = 4096
D = 256
H = D // P
TILES = N // P
PAIRS = TILES // 2
CHUNK = 1024
CHUNKS = N // CHUNK
BANK = 512
GROUP = 4
GROUPS = TILES // GROUP
RING = 3
SLAB = 4
SCALE = float(D) ** -0.5
EPS = 1e-5
MASKED = (-1e9, -1e30)
FLOOR = -1e29
TINY = 1e-30
EPI_STEPS = (7, 3)
BODY = 2 * SLAB


class Tile:

    def __init__(self, layer, pair, par):
        self.layer, self.pair, self.par = layer, pair, par
        self.n = pair * 2 + (TILES * layer + par)

    def after(self, k):
        q = self.par + k
        return Tile(self.layer, self.pair + q // 2, q % 2)

    def loads(self, dmas=1):
        return (self.pair + (PAIRS * self.layer + 1)) * (16 * dmas)

    def layer_loads(self, dmas=1):
        return (self.pair + 1) * (16 * dmas)


def loop(eng, layer, count, body):
    if layer == 0:
        body(0)
    with eng.Fori(1 - layer, count) as i:
        body(i)


def wait_used(eng, sem, value):
    if not isinstance(value, int) or value > 0:
        eng.wait_ge(sem, value)


def steps(eng, layer, step):
    first = Tile(layer, 0, 0)
    step(None, first, first.after(1))

    def body(pair):
        for par in range(2):
            cur = Tile(layer, pair, par)
            step(cur, cur.after(1), cur.after(2))

    loop(eng, layer, PAIRS - 1, body)
    cur = Tile(layer, PAIRS - 1, 0)
    step(cur, cur.after(1), None)
    step(cur.after(1), None, None)


def adj_resnorm(nc, a, out):
    with ExitStack() as ctx:
        def sem(name):
            return ctx.enter_context(nc.semaphore(name))

        size = {F32: 4, F32R: 4, BF16: 2, U8: 1, U16: 2}
        top = [-(-nc.sbuf_base // 32) * 32]

        def place(name, shape, dt, at=None):
            nbytes = size[dt]
            for d in shape[1:]:
                nbytes *= d
            where = top if at is None else at
            t = nc.alloc_sbuf_tensor_at(name, shape, dt, offset=where[0])
            where[0] += -(-nbytes // 32) * 32
            return t

        keys_hi = place("keys_hi", [P, H, N], F32R)
        keys_lo = place("keys_lo", [P, H, N], F32R)
        values_at = list(top)
        values = place("values", [P, TILES, 2 * D], F32R)
        probs_at = list(top)
        probs = place("probs", [P, 2, N], F32)
        ring_at = list(top)
        pt_hi = place("pt_hi", [P, RING, BANK], F32R)
        pt_lo = place("pt_lo", [P, RING, BANK], F32R)
        adj8 = place("adj8", [P, 2 * N], U8)
        mask = place("mask", [P, CHUNKS, CHUNK], BF16)
        q_split = place("q_split", [P, 2, 2, H, P], F32R)
        r_split = place("r_split", [P, 2, 2, H, P], F32R)
        rows_q = place("rows_q", [P, 2, D], F32)
        rows_max = place("rows_max", [P, 2, D], F32)
        rows_res = place("rows_res", [P, 2, D], F32)
        edge_v = place("edge_v", [P, 2, D], F32)
        out_rows = place("out_rows", [P, 2, D], F32)
        y_tmp = place("y_tmp", [P, D], F32)
        dot_out = place("dot_out", [P, D], F32)
        w_ev = place("w_ev", [P, 2, H, D], F32R)
        w_q = place("w_q", [P, 2, H, D], F32R)
        ident = place("ident", [P, P], F32)
        u_bc = place("u_bc", [P, D], F32)
        wes_bc = place("wes_bc", [P, D], F32)
        gv_bc = place("gv_bc", [P, D], F32)
        bev_bc = place("bev_bc", [P, D], F32)
        row_max = place("row_max", [P, 2, 6], F32)
        neg_max = place("neg_max", [P, 2], F32)
        sums = place("sums", [P, 2, 5], F32)
        ge_exp = place("ge_exp", [P, 2, 2], F32)
        ge_w = place("ge_w", [P, 2], F32)
        den = place("den", [P, 2], F32)
        rden = place("rden", [P, 1], F32)
        stats = place("stats", [P, 6], F32)
        mean_var = place("mean_var", [P, 2, 2], F32)
        var_eps = place("var_eps", [P, 1], F32)
        rstd = place("rstd", [P, 1], F32)
        minus_half = place("minus_half", [P, 1], F32)
        eps = place("eps", [P, 1], F32)
        w_v = place("w_v", [P, 2, H, D], F32R, probs_at)
        w_v1 = place("w_v1", [P, 2, H, D], F32R, probs_at)
        w_q1 = place("w_q1", [P, 2, H, D], F32R, probs_at)
        slab = place("slab", [P, 2, SLAB, D], F32, probs_at)
        x_hi = place("x_hi", [P, 2, H, P], F32R, probs_at)
        x_lo = place("x_lo", [P, 2, H, P], F32R, probs_at)
        blv = place("blv", [1, D], F32, probs_at)
        blv_hi = place("blv_hi", [1, D], F32R, probs_at)
        blv_lo = place("blv_lo", [1, D], F32R, probs_at)
        ones = place("ones", [1, P], F32R, probs_at)
        x_sums = place("x_sums", [P, TILES, H], F32, probs_at)
        wgk = place("wgk", [P, H, D], F32, ring_at)
        wgv = place("wgv", [P, H, D], F32, ring_at)
        wgq_t = place("wgq_t", [P, H, D], F32, ring_at)
        x_bar = place("x_bar", [P, H, P], F32, ring_at)
        gk = place("gk", [P, H, P], F32, ring_at)
        x_total = place("x_total", [P, H], F32, ring_at)
        ones_f = place("ones_f", [P, P], F32, ring_at)
        raw = {w: place(f"raw_{w}", [P, H, D], F32, values_at)
               for w in ("Wlq", "Wlk", "Wgq", "Wlv", "Wev", "Wq", "Wk", "Wv")}
        wlq_t = place("wlq_t", [P, H, D], F32, values_at)
        wlk_t = place("wlk_t", [P, H, D], F32, values_at)

        def psum(name, cols):
            return ctx.enter_context(nc.psum_tensor(name, [P, cols], F32))

        ps_scores = [psum(f"ps_scores{i}", CHUNK) for i in range(2)]
        ps_t = [psum(f"ps_t{i}", BANK) for i in range(2)]
        ps_out = psum("ps_out", BANK)
        ps_proj = psum("ps_proj", BANK)
        ps_value = [ps_scores[0][:, 0:D], ps_scores[1][:, 0:D]]

        x1 = nc.dram_tensor("x1_rows", (N, D), F32).ap()
        w1_kept = nc.dram_tensor("w1_kept", (2, P, 2 * H * D), F32).ap()
        x1_pairs = x1.rearrange("(n two) d -> n (two d)", two=2)
        out_pairs = out.rearrange("(n two) d -> n (two d)", two=2)
        adj16 = a["adj"].bitcast(U16)
        masked_x, x = a["L0_gnn_masked_x"], a["x"]

        weights_in = sem("weights_in")
        biases_in = sem("biases_in")
        slab_in = [sem(f"slab_in{i}") for i in range(2)]
        rows_q_in = [sem(f"rows_q_in{i}") for i in range(2)]
        rows_res_in = [[sem(f"rows_res_in{l}{i}") for i in range(2)] for l in range(2)]
        adj_in = [sem(f"adj_in{i}") for i in range(2)]
        adj_t_in = [sem(f"adj_t_in{c}") for c in range(CHUNKS)]
        stored = [sem(f"stored{i}") for i in range(2)]
        const_set = sem("const_set")
        ident_set = sem("ident_set")
        ones_set = sem("ones_set")
        floor_set = sem("floor_set")
        w1_out = sem("w1_out")
        w1_in = sem("w1_in")
        setup_mm = sem("setup_mm")
        setup_hi = sem("setup_hi")
        setup_lo = sem("setup_lo")
        xt_mm = sem("xt_mm")
        xt_hi = sem("xt_hi")
        xt_lo = sem("xt_lo")
        xt_kept = sem("xt_kept")
        value_mm = sem("value_mm")
        value_hi = sem("value_hi")
        value_lo = sem("value_lo")
        x_summed = sem("x_summed")
        mean_step = sem("mean_step")
        global_mm = sem("global_mm")
        global_set = sem("global_set")
        rt_mm = sem("rt_mm")
        rt_hi = sem("rt_hi")
        rt_lo = sem("rt_lo")
        q_mm = sem("q_mm")
        q_hi = sem("q_hi")
        q_lo = sem("q_lo")
        edge_mm = sem("edge_mm")
        edge_set = sem("edge_set")
        global_dot = sem("global_dot")
        edge_dot = sem("edge_dot")
        scores_mm = sem("scores_mm")
        mask_set = sem("mask_set")
        masked = sem("masked")
        max_set = sem("max_set")
        exped = sem("exped")
        pt_mm = sem("pt_mm")
        pt_hi_set = sem("pt_hi_set")
        pt_lo_set = sem("pt_lo_set")
        pv_mm = sem("pv_mm")
        sums_used = sem("sums_used")
        out_read = sem("out_read")
        epi_step = sem("epi_step")
        stats_set = sem("stats_set")
        var_step = sem("var_step")
        normed = sem("normed")

        values_flat = values[:].rearrange("p t d -> p (t d)")

        def f32(t):
            return t.bitcast(F32)

        block = ctx.enter_context(nc.Block())

        @block.sync
        def _(sp):
            def w_rows(w):
                return w.rearrange("(h p) d -> p h d", p=P)

            for w in ("Wlq", "Wlk", "Wgq", "Wlv", "Wev"):
                sp.dma_start(raw[w][:], w_rows(a["L0_gnn_" + w])).then_inc(weights_in, 16)
            for w in ("Wq", "Wk", "Wv"):
                sp.dma_start(raw[w][:], w_rows(a["L1_gnn_" + w])).then_inc(weights_in, 16)
            sp.dma_start(blv[:], a["L0_gnn_blv"].rearrange("(o d) -> o d", o=1)).then_inc(weights_in, 16)

            def load_slabs(layer, rows, end, start=0):
                view = rows.rearrange("(g s p) d -> g p s d", s=SLAB, p=P)
                for g in range(start, end):
                    if g >= 2:
                        sp.wait_ge(xt_mm, TILES * layer + SLAB * (g - 1))
                    sp.dma_start(slab[:, g % 2], view[g]).then_inc(slab_in[g % 2], 16)

            flat = "p k h d -> p (k h d)"
            load_slabs(0, x, 2)
            sp.wait_ge(setup_lo, 7)
            sp.dma_start(w1_kept[0], f32(w_v1[:]).rearrange(flat)).then_inc(w1_out, 16)
            sp.dma_start(w1_kept[1], f32(w_q1[:]).rearrange(flat)).then_inc(w1_out, 16)
            load_slabs(0, x, TILES // SLAB, 2)
            sp.dma_start(wgk[:], w_rows(a["L0_gnn_Wgk"])).then_inc(biases_in, 16)
            sp.dma_start(wgv[:], w_rows(a["L0_gnn_Wgv"])).then_inc(biases_in, 16)
            for t, name in ((gv_bc, "bgv"), (bev_bc, "bev")):
                row = a["L0_gnn_" + name].rearrange("(o d) -> o d", o=1)
                sp.dma_start(t[:], row.to_broadcast([P, D])).then_inc(biases_in, 16)
            sp.dma_start(wes_bc[:], a["L0_gnn_Wes"].rearrange("d o -> o d").to_broadcast([P, D])).then_inc(biases_in, 16)

            def load_rows_q(t):
                if t.layer == 0:
                    sp.dma_start(rows_q[:, t.par], masked_x[bass.ds(t.n * P, P), :]).then_inc(rows_q_in[t.par], 16)
                else:
                    sp.dma_start(rows_q[:, t.par], x1_pairs[bass.ds(t.pair * P, P), t.par * D:(t.par + 1) * D]
                                 ).then_inc(rows_q_in[t.par], 16)

            def load_rows_res(t):
                s = rows_res_in[t.layer][t.par]
                if t.layer == 0:
                    sp.dma_start(rows_max[:, t.par], masked_x[bass.ds(t.n * P, P), :]).then_inc(s, 16)
                    sp.dma_start(rows_res[:, t.par], x[bass.ds(t.n * P, P), :]).then_inc(s, 16)
                else:
                    sp.dma_start(rows_max[:, t.par], x1_pairs[bass.ds(t.pair * P, P), t.par * D:(t.par + 1) * D]
                                 ).then_inc(s, 16)

            def load_adj(t):
                sp.dma_start(adj8[:, t.par * N:(t.par + 1) * N], a["adj"][bass.ds(t.n * P, P), :]
                             ).then_inc(adj_in[t.par], 16)

            def load_adj_t(t, c):
                sp.dma_start_transpose(adj8.bitcast(U16)[:, c * CHUNK:(c + 1) * CHUNK],
                                       adj16[c * CHUNK:(c + 1) * CHUNK, bass.ds(t.pair * P, P)]
                                       ).then_inc(adj_t_in[c], 16)

            for layer in range(2):
                first = Tile(layer, 0, 0)
                if layer == 1:
                    sp.wait_ge(mask_set, CHUNKS * TILES)
                    for c in range(CHUNKS):
                        load_adj_t(first, c)
                    for par in range(2):
                        sp.wait_ge(stored[par], 16 * PAIRS)
                    sp.wait_ge(w1_out, 32)
                    sp.dma_start(f32(w_v[:]).rearrange(flat), w1_kept[0]).then_inc(w1_in, 16)
                    sp.dma_start(f32(w_q[:]).rearrange(flat), w1_kept[1]).then_inc(w1_in, 16)
                    load_slabs(1, x1, TILES // SLAB)
                load_rows_q(first)
                load_rows_res(first)
                if layer == 0:
                    load_adj(first)

                def step(cur, nxt, far):
                    if far is not None:
                        if layer == 0:
                            if cur is not None:
                                sp.wait_ge(mask_set, far.n * CHUNKS - CHUNKS)
                            load_adj(far)
                        elif far.par == 0:
                            sp.wait_ge(mask_set, far.n * CHUNKS)
                            for c in range(CHUNKS):
                                load_adj_t(far, c)
                        if cur is not None or layer == 1:
                            sp.wait_ge(rt_mm, far.n - 1)
                        if cur is not None and layer == 0:
                            sp.wait_ge(global_dot, far.n - 1)
                            sp.wait_ge(edge_dot, far.n - 1)
                        load_rows_q(far)
                    if nxt is not None and cur is not None:
                        wait_used(sp, normed, nxt.n - 1)
                        load_rows_res(nxt)

                steps(sp, layer, step)

        @block.gpsimd
        def _(pool):
            nc.gpsimd.memset(ident[:], 0.0).then_inc(const_set, 1)
            pool.wait_ge(const_set, 1)
            nc.gpsimd.affine_select(out=ident[:], in_=ident[:], compare_op=ALU.not_equal, fill=1.0, base=0,
                                    pattern=[[-1, P]], channel_multiplier=1).then_inc(ident_set, 1)
            nc.gpsimd.memset(ones_f[:], 1.0).then_inc(ones_set, 1)
            nc.gpsimd.memset(f32(ones[:]), 1.0).then_inc(ones_set, 1)
            nc.gpsimd.memset(minus_half[:], -0.5).then_inc(const_set, 1)
            nc.gpsimd.memset(eps[:], EPS).then_inc(const_set, 1)
            pool.wait_ge(const_set, 3)

            def norm(t):
                pool.wait_ge(stats_set, t.n + 1)
                nc.gpsimd.tensor_tensor(var_eps[:], mean_var[:, t.par, 1:2], eps[:], ALU.add).then_inc(var_step, 1)
                wait_used(pool, stored[t.par], t.loads() - 16)
                pool.wait_ge(var_step, t.n + 1)
                nc.gpsimd.tensor_tensor(rstd[:], var_eps[:], minus_half[:], ALU.pow)
                pool.drain()
                nc.gpsimd.tensor_scalar(out_rows[:, t.par], rows_res[:, t.par], mean_var[:, t.par, 0:1], rstd[:],
                                        ALU.subtract, ALU.mult).then_inc(normed, 1)
                pool.wait_ge(normed, t.n + 1)
                if t.layer == 0:
                    to = x1[bass.ds(t.n * P, P), :]
                else:
                    to = out_pairs[bass.ds(t.pair * P, P), t.par * D:(t.par + 1) * D]
                nc.gpsimd.dma_start(to, out_rows[:, t.par]).then_inc(stored[t.par], 16)

            def step(cur, nxt, far):
                if cur is not None:
                    norm(cur)

            for layer in range(2):
                def body(i):
                    for b in range(BODY):
                        j, s = i * BODY + b, b % 2
                        pool.wait_ge(xt_lo, j + (TILES * layer + 1))
                        nc.gpsimd.tensor_copy(keys_hi[:, :, bass.ds(j * P, P)], f32(x_hi[:, s])).then_inc(xt_kept, 1)
                        nc.gpsimd.tensor_copy(keys_lo[:, :, bass.ds(j * P, P)], f32(x_lo[:, s])).then_inc(xt_kept, 1)

                loop(pool, layer, TILES // BODY, body)
                steps(pool, layer, step)
            for par in range(2):
                pool.wait_ge(stored[par], 2 * 16 * PAIRS)

        @block.tensor
        def _(pe):
            def split_mm(dst, lhs, rhs, start=True, stop=True):
                terms = [(h, i, j) for h in range(H) for i, j in ((0, 0), (0, 1), (1, 0))]
                for n, (h, i, j) in enumerate(terms):
                    last = nc.tensor.matmul(dst, lhs(i, h), rhs(j, h), start=start and n == 0,
                                            stop=stop and n == len(terms) - 1)
                return last

            def transpose_w(dst, w):
                for h in range(H):
                    for k in range(H):
                        last = nc.tensor.transpose(dst[:, h * D + k * P:h * D + k * P + P],
                                                   w[:, k, h * P:(h + 1) * P], ident[:])
                return last

            pe.wait_ge(ident_set, 1)
            pe.wait_ge(weights_in, 16 * 9)
            transpose_w(ps_t[0], raw["Wlq"]).then_inc(setup_mm, 1)
            transpose_w(ps_t[1], raw["Wlk"]).then_inc(setup_mm, 1)
            transpose_w(ps_out, raw["Wgq"]).then_inc(setup_mm, 1)
            transpose_w(ps_proj, raw["Wv"]).then_inc(setup_mm, 1)
            for h in range(H):
                for k in range(H):
                    last = nc.tensor.matmul(ps_scores[0][:, h * D:(h + 1) * D], raw["Wq"][:, k, h * P:(h + 1) * P],
                                            raw["Wk"][:, k, :], start=k == 0, stop=k == H - 1)
            last.then_inc(setup_mm, 1)
            pe.wait_ge(setup_lo, 2)
            for h in range(H):
                for k in range(H):
                    last = nc.tensor.matmul(ps_scores[1][:, h * D:(h + 1) * D], wlq_t[:, k, h * P:(h + 1) * P],
                                            wlk_t[:, k, :], start=k == 0, stop=k == H - 1)
            last.then_inc(setup_mm, 1)
            pe.wait_ge(setup_lo, 8)
            pe.wait_ge(ones_set, 2)

            def key_transposes(layer, i, b):
                if b % SLAB == 0:
                    pe.wait_ge(slab_in[b // SLAB], (i + (TILES // SLAB // 2 * layer + 1)) * 16)
                for h in range(H):
                    last = nc.tensor.transpose(ps_t[b % 2][:, h * P:(h + 1) * P],
                                               slab[:, b // SLAB, b % SLAB, h * P:(h + 1) * P], ident[:])
                last.then_inc(xt_mm, 1)

            def value_product(layer, i, b):
                s = b % 2
                wait_used(pe, value_lo, i * BODY + (TILES * layer + max(b - 1, 0)))
                last = split_mm(ps_value[s], lambda k, h: (x_hi, x_lo)[k][:, s, h],
                                lambda k, h: w_v[:, k, h], stop=layer == 1)
                if layer == 0:
                    nc.tensor.matmul(ps_value[s], ones[:], blv_hi[:], start=False, stop=False)
                    last = nc.tensor.matmul(ps_value[s], ones[:], blv_lo[:], start=False, stop=True)
                last.then_inc(value_mm, 1)

            def key_value_tiles(layer):
                if layer:
                    pe.wait_ge(w1_in, 32)

                def body(i):
                    for b in range(BODY + 1):
                        if b < BODY:
                            key_transposes(layer, i, b)
                        if b >= 1:
                            pe.wait_ge(xt_lo, i * BODY + (TILES * layer + b))
                            value_product(layer, i, b - 1)

                loop(pe, layer, TILES // BODY, body)

            def query_transposes(t):
                pe.wait_ge(rows_q_in[t.par], t.loads())
                for h in range(H):
                    last = nc.tensor.transpose(ps_proj[:, D + h * P:D + (h + 1) * P],
                                               rows_q[:, t.par, h * P:(h + 1) * P], ident[:])
                last.then_inc(rt_mm, 1)

            def query_product(t):
                pe.wait_ge(rt_lo, t.n + 1)
                for half in range(H):
                    last = split_mm(ps_proj[:, half * P:(half + 1) * P],
                                    lambda k, h: w_q[:, k, h, half * P:(half + 1) * P],
                                    lambda k, h: r_split[:, t.par, k, h])
                last.then_inc(q_mm, 1)

            def edge_values(t):
                split_mm(ps_proj[:, 0:D], lambda k, h: r_split[:, t.par, k, h],
                         lambda k, h: w_ev[:, k, h]).then_inc(edge_mm, 1)

            def scores(t, c):
                dst = ps_scores[c % 2]
                for h in range(H):
                    for k, keys in ((0, keys_hi), (0, keys_lo), (1, keys_hi)):
                        for b in range(CHUNK // BANK):
                            col = c * CHUNK + b * BANK
                            last = nc.tensor.matmul(dst[:, b * BANK:(b + 1) * BANK], q_split[:, t.par, k, h],
                                                    keys[:, h, col:col + BANK],
                                                    start=h == 0 and k == 0 and keys is keys_hi,
                                                    stop=h == H - 1 and k == 1, skip_group_check=True)
                last.then_inc(scores_mm, 1)

            def prob_transposes(t, g):
                if g % 2 == 0:
                    pe.wait_ge(exped, t.n * CHUNKS + (g // 2 + 1))
                for b in range(GROUP):
                    col = (g * GROUP + b) * P
                    last = nc.tensor.transpose(ps_t[g % 2][:, b * P:(b + 1) * P], probs[:, t.par, col:col + P],
                                               ident[:])
                last.then_inc(pt_mm, 1)

            def values_product(t, g):
                for b in range(GROUP):
                    j, sl = g * GROUP + b, slice(b * P, (b + 1) * P)
                    nc.tensor.matmul(ps_out[:], pt_hi[:, g % RING, sl], values[:, j, :],
                                     start=j == 0, stop=False, skip_group_check=True)
                    last = nc.tensor.matmul(ps_out[:, 0:D], pt_lo[:, g % RING, sl], values[:, j, 0:D],
                                            start=False, stop=j == TILES - 1, skip_group_check=True)
                last.then_inc(pv_mm, 1)

            def step(cur, nxt, far):
                for c in range(CHUNKS):
                    if c == 3 and cur is not None:
                        prob_transposes(cur, 0)
                        prob_transposes(cur, 1)
                    if nxt is not None:
                        if c == 0:
                            pe.wait_ge(q_lo, nxt.n + 1)
                        if cur is not None or c >= 2 or nxt.layer:
                            pe.wait_ge(masked, nxt.n * CHUNKS + (c - 1))
                        scores(nxt, c)
                    if far is not None and c == 0:
                        pe.wait_ge(q_lo, far.n)
                        if far.layer == 0 and cur is not None:
                            pe.wait_ge(edge_set, cur.n + 1)
                        query_transposes(far)
                    if far is not None and c == 1:
                        query_product(far)
                if cur is None and nxt.layer == 0:
                    pe.wait_ge(q_lo, far.n + 1)
                    edge_values(nxt)
                if cur is not None:
                    for g in range(GROUPS):
                        pe.wait_ge(pt_lo_set, cur.n * GROUPS + (g + 1))
                        if g + 2 < GROUPS:
                            prob_transposes(cur, g + 2)
                        if g == 0:
                            wait_used(pe, out_read, cur.n)
                        values_product(cur, g)
                        if g == 3 and nxt is not None and nxt.layer == 0:
                            pe.wait_ge(q_lo, (far or nxt).n + 1)
                            edge_values(nxt)

            for layer in range(2):
                key_value_tiles(layer)
                if layer == 0:
                    pe.wait_ge(mean_step, 3)
                    pe.wait_ge(biases_in, 16 * 5)
                    for h in range(H):
                        for k in range(H):
                            last = nc.tensor.matmul(ps_proj[:, h * P:(h + 1) * P], wgk[:, k, h * P:(h + 1) * P],
                                                    x_bar[:, k], start=k == 0, stop=k == H - 1)
                    last.then_inc(global_mm, 1)
                    for k in range(H):
                        last = nc.tensor.matmul(ps_out[:, 0:D], x_bar[:, k], wgv[:, k], start=k == 0, stop=k == H - 1)
                    last.then_inc(global_mm, 1)
                    pe.wait_ge(global_set, 1)
                    for k in range(H):
                        last = nc.tensor.matmul(ps_t[0][:, 0:D], gk[:, k], wgq_t[:, k], start=k == 0, stop=k == H - 1)
                    last.then_inc(global_mm, 1)
                    pe.wait_ge(global_set, 3)
                first = Tile(layer, 0, 0)
                query_transposes(first)
                query_product(first)
                pe.wait_ge(xt_kept, 2 * TILES * (layer + 1))
                pe.wait_ge(value_lo, TILES * (layer + 1))
                steps(pe, layer, step)

        @block.scalar
        def _(act):
            def hi(dst, src, **kw):
                return nc.scalar.activation(dst, src, ACT.Copy, **kw)

            act.wait_ge(weights_in, 16 * 9)
            hi(w_v[:, 0], raw["Wlv"][:]).then_inc(setup_hi, 1)
            hi(w_ev[:, 0], raw["Wev"][:]).then_inc(setup_hi, 1)
            hi(blv_hi[:], blv[:]).then_inc(setup_hi, 1)
            act.wait_ge(setup_mm, 3)
            hi(wgq_t[:], ps_out[:]).then_inc(setup_hi, 1)
            act.wait_ge(setup_mm, 4)
            hi(w_v1[:, 0], ps_proj[:]).then_inc(setup_hi, 1)
            act.wait_ge(setup_mm, 5)
            hi(w_q1[:, 0], ps_scores[0][:, 0:BANK]).then_inc(setup_hi, 1)
            act.wait_ge(setup_mm, 6)
            hi(w_q[:, 0], ps_scores[1][:, 0:BANK], scale=SCALE).then_inc(setup_hi, 1)

            def key_values(layer):
                def body(i):
                    for b in range(BODY + 1):
                        n = i * BODY + (TILES * layer + b)
                        if b < BODY:
                            act.wait_ge(xt_mm, n + 1)
                            used = i * BODY + (TILES * layer + max(b - 1, 0))
                            wait_used(act, xt_kept, used * 2)
                            wait_used(act, value_mm, used)
                            hi(x_hi[:, b % 2], ps_t[b % 2][:, 0:D]).then_inc(xt_hi, 1)
                        if b >= 1:
                            act.wait_ge(value_mm, n)
                            hi(values_flat[:, bass.ds((i * BODY + (b - 1)) * (2 * D), D)], ps_value[(b - 1) % 2]
                               ).then_inc(value_hi, 1)

                loop(act, layer, TILES // BODY, body)

            def mask_chunk(t, c):
                if t.layer == 0:
                    if c == 0:
                        act.wait_ge(adj_in[t.par], t.layer_loads())
                    src = adj8[:, t.par * N + c * CHUNK:t.par * N + (c + 1) * CHUNK]
                else:
                    act.wait_ge(adj_t_in[c], t.layer_loads())
                    src = adj8[:].rearrange("p (j two) -> p two j", two=2)[:, t.par, c * CHUNK:(c + 1) * CHUNK]
                nc.scalar.activation(mask[:, c], src, ACT.Copy, scale=-MASKED[t.layer], bias=MASKED[t.layer]
                                     ).then_inc(mask_set, 1)

            def next_mask(t, c):
                act.wait_ge(masked, t.n * CHUNKS + (c + 1 - CHUNKS))
                mask_chunk(t, c)

            def exp_chunk(t, c):
                if c == 0:
                    act.wait_ge(max_set, t.n + 1)
                    wait_used(act, sums_used, t.n - 1)
                    if t.layer == 0:
                        nc.scalar.activation(ge_exp[:, t.par], row_max[:, t.par, 4:6], ACT.Exp,
                                             bias=neg_max[:, t.par:t.par + 1], accum_out=sums[:, t.par, 4:5])
                chunk = probs[:, t.par, c * CHUNK:(c + 1) * CHUNK]
                nc.scalar.activation(chunk, chunk, ACT.Exp, bias=neg_max[:, t.par:t.par + 1],
                                     accum_out=sums[:, t.par, c:c + 1]).then_inc(exped, 1)

            def query_rows_hi(t):
                act.wait_ge(rt_mm, t.n + 1)
                hi(r_split[:, t.par, 0], ps_proj[:, D:2 * D]).then_inc(rt_hi, 1)

            def query_hi(t):
                act.wait_ge(q_mm, t.n + 1)
                hi(q_split[:, t.par, 0], ps_proj[:, 0:D]).then_inc(q_hi, 1)

            def prob_hi(t, g):
                act.wait_ge(pt_mm, t.n * GROUPS + (g + 1))
                if g < RING:
                    wait_used(act, out_read, t.n)
                else:
                    act.wait_ge(pv_mm, t.n * GROUPS + (g + 1 - RING))
                hi(pt_hi[:, g % RING], ps_t[g % 2][:]).then_inc(pt_hi_set, 1)

            def step(cur, nxt, far):
                if cur is not None:
                    exp_chunk(cur, 2)
                    exp_chunk(cur, 3)
                if far is not None:
                    query_rows_hi(far)
                    next_mask(far, 0)
                    query_hi(far)
                    next_mask(far, 1)
                if cur is not None:
                    prob_hi(cur, 0)
                    prob_hi(cur, 1)
                if far is not None:
                    next_mask(far, 2)
                if cur is not None:
                    prob_hi(cur, 2)
                if far is not None:
                    next_mask(far, 3)
                if cur is not None:
                    prob_hi(cur, 3)
                if nxt is not None:
                    exp_chunk(nxt, 0)
                if cur is not None:
                    prob_hi(cur, 4)
                if nxt is not None:
                    exp_chunk(nxt, 1)
                if cur is not None:
                    for g in range(5, GROUPS):
                        prob_hi(cur, g)

            for layer in range(2):
                key_values(layer)
                first = Tile(layer, 0, 0)
                for c in range(CHUNKS):
                    if layer:
                        next_mask(first, c)
                    else:
                        mask_chunk(first, c)
                query_rows_hi(first)
                query_hi(first)
                steps(act, layer, step)

        @block.vector
        def _(dve):
            def lo(dst, src, hi_half):
                return nc.vector.tensor_tensor(dst, src, f32(hi_half), ALU.subtract)

            dve.wait_ge(setup_mm, 1)
            nc.vector.tensor_copy(wlq_t[:], ps_t[0][:]).then_inc(setup_lo, 1)
            dve.wait_ge(setup_mm, 2)
            nc.vector.tensor_copy(wlk_t[:], ps_t[1][:]).then_inc(setup_lo, 1)
            dve.wait_ge(setup_hi, 3)
            lo(w_v[:, 1], raw["Wlv"][:], w_v[:, 0]).then_inc(setup_lo, 1)
            lo(w_ev[:, 1], raw["Wev"][:], w_ev[:, 0]).then_inc(setup_lo, 1)
            lo(blv_lo[:], blv[:], blv_hi[:]).then_inc(setup_lo, 1)
            dve.wait_ge(setup_hi, 5)
            lo(w_v1[:, 1], ps_proj[:], w_v1[:, 0]).then_inc(setup_lo, 1)
            dve.wait_ge(setup_hi, 6)
            lo(w_q1[:, 1], ps_scores[0][:, 0:BANK], w_q1[:, 0]).then_inc(setup_lo, 1)
            dve.wait_ge(setup_hi, 7)
            nc.vector.scalar_tensor_tensor(out=w_q[:, 1], in0=ps_scores[1][:, 0:BANK], scalar=SCALE,
                                           in1=f32(w_q[:, 0]), op0=ALU.mult, op1=ALU.subtract).then_inc(setup_lo, 1)

            def key_values(layer):
                def body(i):
                    for b in range(BODY + 1):
                        n = i * BODY + (TILES * layer + b)
                        if b < BODY:
                            dve.wait_ge(xt_hi, n + 1)
                            if layer == 0:
                                nc.vector.tensor_reduce(x_sums[:, bass.ds(i * BODY + b, 1), :].rearrange("p o h -> p (o h)"),
                                                        ps_t[b % 2][:, 0:D].rearrange("p (h j) -> p h j", h=H),
                                                        AX.X, ALU.add).then_inc(x_summed, 1)
                            lo(x_lo[:, b % 2], ps_t[b % 2][:, 0:D], x_hi[:, b % 2]).then_inc(xt_lo, 1)
                        if b >= 1:
                            dve.wait_ge(value_hi, n)
                            at = (i * BODY + (b - 1)) * (2 * D)
                            lo(values_flat[:, bass.ds(at + D, D)], ps_value[(b - 1) % 2],
                               values_flat[:, bass.ds(at, D)]).then_inc(value_lo, 1)

                loop(dve, layer, TILES // BODY, body)

            def global_terms():
                dve.wait_ge(x_summed, TILES)
                nc.vector.tensor_reduce(x_total[:], x_sums[:].rearrange("p j h -> p h j"), AX.X, ALU.add
                                        ).then_inc(mean_step, 1)
                dve.wait_ge(mean_step, 1)
                dve.wait_ge(ones_set, 1)
                for h in range(H):
                    nc.vector.tensor_scalar(x_bar[:, h], ones_f[:], x_total[:, h:h + 1], 1.0 / N, ALU.mult, ALU.mult
                                            ).then_inc(mean_step, 1)
                dve.wait_ge(global_mm, 1)
                nc.vector.tensor_copy(gk[:], ps_proj[:, 0:D]).then_inc(global_set, 1)
                dve.wait_ge(biases_in, 16 * 5)
                dve.wait_ge(global_mm, 2)
                nc.vector.tensor_tensor(gv_bc[:], ps_out[:, 0:D], gv_bc[:], ALU.add).then_inc(global_set, 1)
                dve.wait_ge(global_mm, 3)
                nc.vector.tensor_scalar(u_bc[:], ps_t[0][:, 0:D], SCALE, None, ALU.mult).then_inc(global_set, 1)
                dve.wait_ge(global_set, 3)

            def row_dots(t):
                dve.wait_ge(rows_q_in[t.par], t.loads())
                wait_used(dve, exped, t.n * CHUNKS + (1 - 2 * CHUNKS))
                for k, vec, dot in ((0, u_bc, global_dot), (1, wes_bc, edge_dot)):
                    nc.vector.tensor_tensor_reduce(out=dot_out[:], in0=rows_q[:, t.par], in1=vec[:], scale=1.0,
                                                   scalar=0.0, op0=ALU.mult, op1=ALU.add,
                                                   accum_out=row_max[:, t.par, 4 + k:5 + k]).then_inc(dot, 1)
                    dve.wait_ge(dot, t.n + 1)

            def query_rows_lo(t):
                dve.wait_ge(rt_hi, t.n + 1)
                lo(r_split[:, t.par, 1], ps_proj[:, D:2 * D], r_split[:, t.par, 0]).then_inc(rt_lo, 1)

            def query_lo(t):
                dve.wait_ge(q_hi, t.n + 1)
                lo(q_split[:, t.par, 1], ps_proj[:, 0:D], q_split[:, t.par, 0]).then_inc(q_lo, 1)

            def edge_rows(t):
                dve.wait_ge(edge_mm, t.n + 1)
                nc.vector.tensor_tensor(edge_v[:, t.par], ps_proj[:, 0:D], bev_bc[:], ALU.add).then_inc(edge_set, 1)

            def mask_scores(t, c):
                count = dve.compute_val(t.n * CHUNKS + (c + 1))
                dve.wait_ge(xt_kept, 2 * TILES * (t.layer + 1))
                dve.wait_ge(mask_set, count)
                dve.wait_ge(scores_mm, count)
                nc.vector.tensor_tensor_reduce(out=probs[:, t.par, c * CHUNK:(c + 1) * CHUNK], in0=ps_scores[c % 2][:],
                                               in1=mask[:, c], scale=1.0, scalar=-3e38, op0=ALU.add, op1=ALU.max,
                                               accum_out=row_max[:, t.par, c:c + 1]).then_inc(masked, 1)

            def set_max(t):
                dve.wait_ge(masked, t.n * CHUNKS + CHUNKS)
                wait_used(dve, exped, t.n * CHUNKS - CHUNKS)
                nc.vector.tensor_reduce(neg_max[:, t.par:t.par + 1], row_max[:, t.par, 0:6 if t.layer == 0 else 5],
                                        AX.X, ALU.max, negate=True).then_inc(max_set, 1)

            def prob_lo(t, g):
                dve.wait_ge(pt_hi_set, t.n * GROUPS + (g + 1))
                lo(pt_lo[:, g % RING], ps_t[g % 2][:], pt_hi[:, g % RING]).then_inc(pt_lo_set, 1)

            def epilogue(t):
                if t.layer == 0:
                    before = t.n * EPI_STEPS[0]
                else:
                    before = t.n * EPI_STEPS[1] + TILES * (EPI_STEPS[0] - EPI_STEPS[1])
                done = [0]

                def then(ins):
                    done[0] += 1
                    ins.then_inc(epi_step, 1)
                    dve.wait_ge(epi_step, before + done[0])

                p = t.par
                d, r = den[:, p:p + 1], rden[:, 0:1]
                dve.wait_ge(exped, t.n * CHUNKS + CHUNKS)
                if t.layer == 0:
                    then(nc.vector.reduce_sum(d, sums[:, p, 0:5], AX.X))
                    then(nc.vector.reciprocal(r, d))
                    nc.vector.tensor_scalar(ge_w[:], ge_exp[:, p], r, None, ALU.mult).then_inc(sums_used, 1)
                    dve.wait_ge(sums_used, t.n + 1)
                    then(nc.vector.tensor_scalar(y_tmp[:], gv_bc[:], ge_w[:, 0:1], None, ALU.mult))
                    dve.wait_ge(edge_set, t.n + 1)
                    then(nc.vector.scalar_tensor_tensor(out=y_tmp[:], in0=edge_v[:, p], scalar=ge_w[:, 1:2],
                                                        in1=y_tmp[:], op0=ALU.mult, op1=ALU.add))
                    add = y_tmp[:]
                    dve.wait_ge(rows_res_in[0][p], t.layer_loads(2))
                else:
                    nc.vector.reduce_sum(d, sums[:, p, 0:4], AX.X).then_inc(sums_used, 1)
                    dve.wait_ge(sums_used, t.n + 1)
                    then(nc.vector.tensor_scalar(d, d, TINY, None, ALU.max))
                    then(nc.vector.reciprocal(r, d))
                    add = rows_max[:, p]
                    dve.wait_ge(rows_res_in[1][p], t.layer_loads())
                    dve.wait_ge(normed, t.n - 1)
                dve.wait_ge(pv_mm, t.n * GROUPS + GROUPS)
                then(nc.vector.scalar_tensor_tensor(out=y_tmp[:], in0=ps_out[:, 0:D], scalar=r, in1=add,
                                                    op0=ALU.mult, op1=ALU.add))
                out_t = y_tmp[:] if t.layer == 0 else rows_res[:, p]
                nc.vector.scalar_tensor_tensor(out=out_t, in0=ps_out[:, D:2 * D], scalar=r, in1=y_tmp[:],
                                               op0=ALU.mult, op1=ALU.add).then_inc(out_read, 1)
                dve.wait_ge(out_read, t.n + 1)
                if t.layer == 0:
                    then(nc.vector.tensor_tensor(y_tmp[:], y_tmp[:], rows_max[:, p], ALU.max))
                    then(nc.vector.tensor_tensor(rows_res[:, p], y_tmp[:], rows_res[:, p], ALU.add))
                nc.vector.bn_stats(stats[:], rows_res[:, p])
                dve.drain()
                nc.vector.bn_aggr(mean_var[:, p], stats[:]).then_inc(stats_set, 1)
                assert done[0] == EPI_STEPS[t.layer]

            def step(cur, nxt, far):
                if far is not None:
                    query_rows_lo(far)
                if nxt is not None:
                    mask_scores(nxt, 0)
                    mask_scores(nxt, 1)
                if far is not None:
                    query_lo(far)
                if nxt is not None:
                    mask_scores(nxt, 2)
                if cur is not None:
                    prob_lo(cur, 0)
                    prob_lo(cur, 1)
                if nxt is not None:
                    mask_scores(nxt, 3)
                    set_max(nxt)
                if far is not None and far.layer == 0:
                    row_dots(far)
                if cur is None and nxt.layer == 0:
                    edge_rows(nxt)
                if cur is not None:
                    for g in range(2, GROUPS):
                        prob_lo(cur, g)
                        if g == 5 and nxt is not None and nxt.layer == 0:
                            edge_rows(nxt)
                    epilogue(cur)

            for layer in range(2):
                key_values(layer)
                first = Tile(layer, 0, 0)
                if layer == 0:
                    global_terms()
                    row_dots(first)
                    dve.wait_ge(w1_out, 32)
                else:
                    for par in range(2):
                        nc.vector.memset(row_max[:, par, 4:5], FLOOR).then_inc(floor_set, 1)
                    dve.wait_ge(floor_set, 2)
                query_rows_lo(first)
                query_lo(first)
                steps(dve, layer, step)


_INS = ['x', 'adj', 'L0_gnn_masked_x', 'L0_gnn_Wlq', 'L0_gnn_Wlk', 'L0_gnn_Wlv', 'L0_gnn_blv', 'L0_gnn_Wgq',
        'L0_gnn_Wgk', 'L0_gnn_Wgv', 'L0_gnn_bgv', 'L0_gnn_Wes', 'L0_gnn_Wev', 'L0_gnn_bev', 'L1_gnn_Wq',
        'L1_gnn_Wk', 'L1_gnn_Wv']


def kernel(**inputs):
    import numpy as _np
    import concourse.bacc as _bacc
    from concourse import mybir as _mybir
    from concourse.bass_utils import run_bass_kernel_spmd as _run

    nc = _bacc.Bacc("TRN2", target_bir_lowering=False, num_devices=1, dynamic_dma_scratch_size=1024)
    arrays, args = {}, {}
    for name in _INS:
        arr = _np.ascontiguousarray(inputs[name])
        arrays[f"in_{name}_dram"] = arr
        args[name] = nc.dram_tensor(f"in_{name}_dram", arr.shape, _mybir.dt.from_np(arr.dtype),
                                    kind="ExternalInput").ap()
    out = nc.dram_tensor("out_dram", (N, D), _mybir.dt.float32, kind="ExternalOutput").ap()
    adj_resnorm(nc, args, out)
    r = _run(nc, [arrays], core_ids=[0])
    return r.results[0]["out_dram"]
```

```python
from contextlib import ExitStack

import concourse.bass as bass
from concourse import mybir

F32 = mybir.dt.float32
F32R = mybir.dt.float32r
BF16 = mybir.dt.bfloat16
U8 = mybir.dt.uint8
U16 = mybir.dt.uint16
ALU = mybir.AluOpType
ACT = mybir.ActivationFunctionType
AX = mybir.AxisListType

P = 128
N = 4096
D = 256
H = D // P
TILES = N // P
PAIRS = TILES // 2
CHUNK = 1024
CHUNKS = N // CHUNK
BANK = 512
GROUP = 4
GROUPS = TILES // GROUP
RING = 3
SLAB = 4
SCALE = float(D) ** -0.5
EPS = 1e-5
MASKED = (-1e9, -1e30)
FLOOR = -1e29
TINY = 1e-30
EPI_STEPS = (7, 3)
UNIT = 2
UNITS = TILES // UNIT
BODY = 2 * SLAB // UNIT


class Tile:

    def __init__(self, layer, pair, par):
        self.layer, self.pair, self.par = layer, pair, par
        self.n = pair * 2 + (TILES * layer + par)
        self.m = pair + PAIRS * layer

    def after(self, k):
        q = self.par + k
        return Tile(self.layer, self.pair + q // 2, q % 2)

    def loads(self, dmas=1):
        return (self.m + 1) * (16 * dmas)

    def layer_loads(self, dmas=1):
        return (self.pair + 1) * (16 * dmas)


class Unit:

    def __init__(self, layer, i, b):
        self.layer, self.i, self.b, self.slot = layer, i, b, b % 2
        self.u = i * BODY + b
        self.n = i * BODY + (UNITS * layer + b)

    def after(self):
        return Unit(self.layer, self.i + (self.b + 1) // BODY, (self.b + 1) % BODY)


def loop(eng, layer, count, body):
    if layer == 0:
        body(0)
    with eng.Fori(1 - layer, count) as i:
        body(i)


def wait_used(eng, sem, value):
    if not isinstance(value, int) or value > 0:
        eng.wait_ge(sem, value)


def steps(eng, layer, step):
    first = Tile(layer, 0, 0)
    step(None, first, first.after(1))

    def body(pair):
        for par in range(2):
            cur = Tile(layer, pair, par)
            step(cur, cur.after(1), cur.after(2))

    loop(eng, layer, PAIRS - 1, body)
    cur = Tile(layer, PAIRS - 1, 0)
    step(cur, cur.after(1), Tile(1, 0, 0) if layer == 0 else None)
    step(cur.after(1), None, None)


def units(eng, layer, step):
    step(Unit(layer, 0, 0), None)

    def body(i):
        for b in range(BODY):
            u = Unit(layer, i, b)
            step(u.after(), u)

    loop(eng, layer, UNITS // BODY - 1, body)
    for b in range(BODY):
        u = Unit(layer, UNITS // BODY - 1, b)
        step(u.after() if b < BODY - 1 else None, u)


def adj_resnorm(nc, a, out):
    with ExitStack() as ctx:
        def sem(name):
            return ctx.enter_context(nc.semaphore(name))

        size = {F32: 4, F32R: 4, BF16: 2, U8: 1, U16: 2}
        top = [-(-nc.sbuf_base // 32) * 32]

        def place(name, shape, dt, at=None):
            nbytes = size[dt]
            for d in shape[1:]:
                nbytes *= d
            where = top if at is None else at
            t = nc.alloc_sbuf_tensor_at(name, shape, dt, offset=where[0])
            where[0] += -(-nbytes // 32) * 32
            return t

        keys_hi = place("keys_hi", [P, H, N], F32R)
        keys_lo = place("keys_lo", [P, H, N], F32R)
        values_at = list(top)
        values = place("values", [P, TILES, 2 * D], F32R)
        probs_at = list(top)
        probs = place("probs", [P, 2, N], F32)
        ring_at = list(top)
        pt_hi = place("pt_hi", [P, RING, BANK], F32R)
        pt_lo = place("pt_lo", [P, RING, BANK], F32R)
        adj8 = place("adj8", [P, 2 * N], U8)
        mask = place("mask", [P, CHUNKS, CHUNK], BF16)
        q_split = place("q_split", [P, 2, H, 2 * P], F32R)
        r_split = place("r_split", [P, 2, H, 2 * P], F32R)
        rows_q = place("rows_q", [P, 2, D], F32)
        rows_max = place("rows_max", [P, 2, D], F32)
        rows_res = place("rows_res", [P, 2, D], F32)
        edge_v = place("edge_v", [P, 2, D], F32)
        out_rows = place("out_rows", [P, 2, D], F32)
        y_tmp = place("y_tmp", [P, D], F32)
        dot_out = place("dot_out", [P, D], F32)
        w_ev = place("w_ev", [P, 2, H, D], F32R)
        w_q = place("w_q", [P, 2, H, D], F32R)
        ident = place("ident", [P, P], F32)
        u_bc = place("u_bc", [P, D], F32)
        wes_bc = place("wes_bc", [P, D], F32)
        gv_bc = place("gv_bc", [P, D], F32)
        bev_bc = place("bev_bc", [P, D], F32)
        row_max = place("row_max", [P, 2, 6], F32)
        neg_max = place("neg_max", [P, 2], F32)
        sums = place("sums", [P, 2, 5], F32)
        ge_exp = place("ge_exp", [P, 2, 2], F32)
        ge_w = place("ge_w", [P, 2], F32)
        den = place("den", [P, 2], F32)
        rden = place("rden", [P, 1], F32)
        stats = place("stats", [P, 6], F32)
        mean_var = place("mean_var", [P, 2, 2], F32)
        var_eps = place("var_eps", [P, 1], F32)
        rstd = place("rstd", [P, 1], F32)
        minus_half = place("minus_half", [P, 1], F32)
        eps = place("eps", [P, 1], F32)
        w_v = place("w_v", [P, 2, H, D], F32R, probs_at)
        slab = place("slab", [P, 2, SLAB, D], F32, probs_at)
        x_hi = place("x_hi", [P, 2, H, UNIT * P], F32R, probs_at)
        x_lo = place("x_lo", [P, 2, H, UNIT * P], F32R, probs_at)
        w_v1 = place("w_v1", [P, 2, H, D], F32R, probs_at)
        w_q1 = place("w_q1", [P, 2, H, D], F32R, probs_at)
        blv = place("blv", [1, D], F32, probs_at)
        blv_hi = place("blv_hi", [1, D], F32R, probs_at)
        blv_lo = place("blv_lo", [1, D], F32R, probs_at)
        ones = place("ones", [1, P], F32R, probs_at)
        wgk = place("wgk", [P, H, D], F32, ring_at)
        wgv = place("wgv", [P, H, D], F32, ring_at)
        wgq_t = place("wgq_t", [P, H, D], F32, ring_at)
        x_bar = place("x_bar", [P, H, P], F32, ring_at)
        gk = place("gk", [P, H, P], F32, ring_at)
        x_total = place("x_total", [P, H], F32, ring_at)
        ones_f = place("ones_f", [P, P], F32, ring_at)
        raw = {w: place(f"raw_{w}", [P, H, D], F32, values_at)
               for w in ("Wlq", "Wlk", "Wgq", "Wlv", "Wev", "Wq", "Wk", "Wv")}
        wlq_t = place("wlq_t", [P, H, D], F32, values_at)
        wlk_t = place("wlk_t", [P, H, D], F32, values_at)

        def psum(name, cols):
            return ctx.enter_context(nc.psum_tensor(name, [P, cols], F32))

        ps_scores = [psum(f"ps_scores{i}", CHUNK) for i in range(2)]
        ps_t = [psum(f"ps_t{i}", BANK) for i in range(2)]
        ps_out = psum("ps_out", BANK)
        ps_proj = psum("ps_proj", BANK)
        ps_value = [ps_scores[s][:, 0:BANK] for s in range(2)]
        ps_sum = [ps_out[:, 0:1], ps_scores[0][:, BANK:BANK + 1]]

        x1 = nc.dram_tensor("x1_rows", (N, D), F32).ap()
        w1_kept = nc.dram_tensor("w1_kept", (2, P, 2 * H * D), F32).ap()
        x1_pairs = x1.rearrange("(n two) d -> n (two d)", two=2)
        out_pairs = out.rearrange("(n two) d -> n (two d)", two=2)
        adj16 = a["adj"].bitcast(U16)
        masked_x, x = a["L0_gnn_masked_x"], a["x"]

        weights_in = [sem(f"weights_in{i}") for i in range(2)]
        biases_in = sem("biases_in")
        slab_in = [sem(f"slab_in{i}") for i in range(2)]
        rows_q_in = sem("rows_q_in")
        rows_res_in = [[sem(f"rows_res_in{l}{i}") for i in range(2)] for l in range(2)]
        adj_in = [sem(f"adj_in{i}") for i in range(2)]
        adj_t_in = [sem(f"adj_t_in{c}") for c in range(CHUNKS)]
        stored = [sem(f"stored{i}") for i in range(2)]
        const_set = sem("const_set")
        ident_set = sem("ident_set")
        ones_set = sem("ones_set")
        floor_set = sem("floor_set")
        w1_out = sem("w1_out")
        w_v1_in = sem("w_v1_in")
        w_q1_in = sem("w_q1_in")
        setup_mm = sem("setup_mm")
        setup_hi = sem("setup_hi")
        setup_lo = sem("setup_lo")
        xt_mm = sem("xt_mm")
        xt_hi = sem("xt_hi")
        xt_lo = sem("xt_lo")
        keys_hi_set = sem("keys_hi_set")
        keys_lo_set = sem("keys_lo_set")
        value_mm = sem("value_mm")
        value_hi = sem("value_hi")
        value_lo = sem("value_lo")
        sums_read = sem("sums_read")
        mean_step = sem("mean_step")
        global_mm = sem("global_mm")
        global_set = sem("global_set")
        rt_mm = sem("rt_mm")
        rt_hi = sem("rt_hi")
        rt_lo = sem("rt_lo")
        q_mm = sem("q_mm")
        q_hi = sem("q_hi")
        q_lo = sem("q_lo")
        edge_mm = sem("edge_mm")
        edge_set = sem("edge_set")
        global_dot = sem("global_dot")
        edge_dot = sem("edge_dot")
        scores_mm = sem("scores_mm")
        mask_set = sem("mask_set")
        masked = sem("masked")
        max_set = sem("max_set")
        exped = sem("exped")
        pt_mm = sem("pt_mm")
        pt_hi_set = sem("pt_hi_set")
        pt_lo_set = sem("pt_lo_set")
        pv_mm = sem("pv_mm")
        sums_used = sem("sums_used")
        out_read = sem("out_read")
        epi_step = sem("epi_step")
        stats_set = sem("stats_set")
        var_step = sem("var_step")
        normed = sem("normed")

        def f32(t):
            return t.bitcast(F32)

        block = ctx.enter_context(nc.Block())

        @block.sync
        def _(sp):
            def w_rows(w):
                return w.rearrange("(h p) d -> p h d", p=P)

            for w in ("Wlq", "Wlk"):
                sp.dma_start(raw[w][:], w_rows(a["L0_gnn_" + w])).then_inc(weights_in[0], 16)
            for w in ("Wgq", "Wlv", "Wev"):
                sp.dma_start(raw[w][:], w_rows(a["L0_gnn_" + w])).then_inc(weights_in[1], 16)
            for w in ("Wv", "Wq", "Wk"):
                sp.dma_start(raw[w][:], w_rows(a["L1_gnn_" + w])).then_inc(weights_in[1], 16)
            sp.dma_start(blv[:], a["L0_gnn_blv"].rearrange("(o d) -> o d", o=1)).then_inc(weights_in[1], 16)

            def load_slabs(layer, rows, end, start=0):
                view = rows.rearrange("(g s p) d -> g p s d", s=SLAB, p=P)
                for g in range(start, end):
                    if g >= 2:
                        sp.wait_ge(xt_mm, UNITS * layer + SLAB // UNIT * (g - 1))
                    if layer == 1:
                        for par in range(2):
                            sp.wait_ge(stored[par], 16 * (SLAB // 2) * (g + 1))
                    sp.dma_start(slab[:, g % 2], view[g]).then_inc(slab_in[g % 2], 16)

            def load_rows_q(t):
                if t.layer == 0:
                    rows = masked_x[bass.ds(t.pair * (2 * P), 2 * P), :].rearrange("(t p) d -> p t d", p=P)
                else:
                    rows = x1_pairs[bass.ds(t.pair * P, P), :].rearrange("p (t d) -> p t d", d=D)
                sp.dma_start(rows_q[:], rows).then_inc(rows_q_in, 16)

            def load_rows_res(t):
                s = rows_res_in[t.layer][t.par]
                if t.layer == 0:
                    sp.dma_start(rows_max[:, t.par], masked_x[bass.ds(t.n * P, P), :]).then_inc(s, 16)
                    sp.dma_start(rows_res[:, t.par], x[bass.ds(t.n * P, P), :]).then_inc(s, 16)
                else:
                    sp.dma_start(rows_max[:, t.par], x1_pairs[bass.ds(t.pair * P, P), t.par * D:(t.par + 1) * D]
                                 ).then_inc(s, 16)

            def load_adj(t):
                sp.dma_start(adj8[:, t.par * N:(t.par + 1) * N], a["adj"][bass.ds(t.n * P, P), :]
                             ).then_inc(adj_in[t.par], 16)

            def load_adj_t(t, c):
                sp.dma_start_transpose(adj8.bitcast(U16)[:, c * CHUNK:(c + 1) * CHUNK],
                                       adj16[c * CHUNK:(c + 1) * CHUNK, bass.ds(t.pair * P, P)]
                                       ).then_inc(adj_t_in[c], 16)

            def step(cur, nxt, far):
                if far is not None:
                    if far.layer == 0:
                        if cur is not None:
                            sp.wait_ge(mask_set, far.n * CHUNKS - CHUNKS)
                        load_adj(far)
                    elif far.par == 0:
                        sp.wait_ge(mask_set, far.n * CHUNKS)
                        for c in range(CHUNKS):
                            load_adj_t(far, c)
                    if far.par == 0:
                        sp.wait_ge(rt_mm, far.m)
                        if cur.layer == 0:
                            sp.wait_ge(global_dot, far.n)
                            sp.wait_ge(edge_dot, far.n)
                        if far.layer != cur.layer:
                            for par in range(2):
                                sp.wait_ge(stored[par], 16)
                        load_rows_q(far)
                if nxt is not None and cur is not None:
                    wait_used(sp, normed, nxt.n - 1)
                    load_rows_res(nxt)
                if far is not None and cur is not None and far.layer != cur.layer:
                    sp.wait_ge(w1_out, 32)
                    sp.wait_ge(q_mm, PAIRS)
                    sp.dma_start(f32(w_q[:]).rearrange(flat), w1_kept[1]).then_inc(w_q1_in, 16)

            flat = "p k h d -> p (k h d)"
            first = Tile(0, 0, 0)
            load_rows_q(first)
            load_slabs(0, x, 2)
            sp.wait_ge(setup_lo, 7)
            sp.dma_start(w1_kept[0], f32(w_v1[:]).rearrange(flat)).then_inc(w1_out, 16)
            sp.dma_start(w1_kept[1], f32(w_q1[:]).rearrange(flat)).then_inc(w1_out, 16)
            load_slabs(0, x, TILES // SLAB, 2)
            sp.dma_start(wgk[:], w_rows(a["L0_gnn_Wgk"])).then_inc(biases_in, 16)
            sp.dma_start(wgv[:], w_rows(a["L0_gnn_Wgv"])).then_inc(biases_in, 16)
            for t, name in ((gv_bc, "bgv"), (bev_bc, "bev")):
                row = a["L0_gnn_" + name].rearrange("(o d) -> o d", o=1)
                sp.dma_start(t[:], row.to_broadcast([P, D])).then_inc(biases_in, 16)
            sp.dma_start(wes_bc[:], a["L0_gnn_Wes"].rearrange("d o -> o d").to_broadcast([P, D])).then_inc(biases_in, 16)
            load_rows_res(first)
            load_adj(first)
            steps(sp, 0, step)

            first = Tile(1, 0, 0)
            sp.wait_ge(pt_mm, (TILES - 1) * GROUPS)
            sp.dma_start(f32(w_v[:]).rearrange(flat), w1_kept[0]).then_inc(w_v1_in, 16)
            load_slabs(1, x1, TILES // SLAB)
            load_rows_res(first)
            steps(sp, 1, step)

        @block.gpsimd
        def _(pool):
            nc.gpsimd.memset(ident[:], 0.0).then_inc(const_set, 1)
            pool.wait_ge(const_set, 1)
            nc.gpsimd.affine_select(out=ident[:], in_=ident[:], compare_op=ALU.not_equal, fill=1.0, base=0,
                                    pattern=[[-1, P]], channel_multiplier=1).then_inc(ident_set, 1)
            nc.gpsimd.memset(ones_f[:], 1.0).then_inc(ones_set, 1)
            nc.gpsimd.memset(f32(ones[:]), 1.0).then_inc(ones_set, 1)
            nc.gpsimd.memset(minus_half[:], -0.5).then_inc(const_set, 1)
            nc.gpsimd.memset(eps[:], EPS).then_inc(const_set, 1)
            pool.wait_ge(const_set, 3)

            def norm(t):
                pool.wait_ge(stats_set, t.n + 1)
                nc.gpsimd.tensor_tensor(var_eps[:], mean_var[:, t.par, 1:2], eps[:], ALU.add).then_inc(var_step, 1)
                wait_used(pool, stored[t.par], t.loads() - 16)
                pool.wait_ge(var_step, t.n + 1)
                nc.gpsimd.tensor_tensor(rstd[:], var_eps[:], minus_half[:], ALU.pow)
                pool.drain()
                nc.gpsimd.tensor_scalar(out_rows[:, t.par], rows_res[:, t.par], mean_var[:, t.par, 0:1], rstd[:],
                                        ALU.subtract, ALU.mult).then_inc(normed, 1)
                pool.wait_ge(normed, t.n + 1)
                if t.layer == 0:
                    to = x1[bass.ds(t.n * P, P), :]
                else:
                    to = out_pairs[bass.ds(t.pair * P, P), t.par * D:(t.par + 1) * D]
                nc.gpsimd.dma_start(to, out_rows[:, t.par]).then_inc(stored[t.par], 16)

            def step(cur, nxt, far):
                if cur is not None:
                    norm(cur)

            for layer in range(2):
                def keep_lo(t, v):
                    if t is not None:
                        pool.wait_ge(xt_lo, t.n + 1)
                        nc.gpsimd.tensor_copy(keys_lo[:, :, bass.ds(t.u * (UNIT * P), UNIT * P)], f32(x_lo[:, t.slot])
                                              ).then_inc(keys_lo_set, 1)

                units(pool, layer, keep_lo)
                steps(pool, layer, step)
            for par in range(2):
                pool.wait_ge(stored[par], 2 * 16 * PAIRS)

        @block.tensor
        def _(pe):
            def split_mm(dst, lhs, rhs, start=True, stop=True):
                terms = [(h, i, j) for h in range(H) for i, j in ((0, 0), (0, 1), (1, 0))]
                for n, (h, i, j) in enumerate(terms):
                    last = nc.tensor.matmul(dst, lhs(i, h), rhs(j, h), start=start and n == 0,
                                            stop=stop and n == len(terms) - 1)
                return last

            def transpose_w(dst, w):
                for h in range(H):
                    for k in range(H):
                        last = nc.tensor.transpose(dst[:, h * D + k * P:h * D + k * P + P],
                                                   w[:, k, h * P:(h + 1) * P], ident[:])
                return last

            pe.wait_ge(ident_set, 1)
            pe.wait_ge(weights_in[0], 16 * 2)
            transpose_w(ps_t[0], raw["Wlq"]).then_inc(setup_mm, 1)
            transpose_w(ps_t[1], raw["Wlk"]).then_inc(setup_mm, 1)
            pe.wait_ge(weights_in[1], 16 * 7)
            transpose_w(ps_out, raw["Wgq"]).then_inc(setup_mm, 1)
            transpose_w(ps_proj, raw["Wv"]).then_inc(setup_mm, 1)
            for h in range(H):
                for k in range(H):
                    last = nc.tensor.matmul(ps_scores[0][:, h * D:(h + 1) * D], raw["Wq"][:, k, h * P:(h + 1) * P],
                                            raw["Wk"][:, k, :], start=k == 0, stop=k == H - 1)
            last.then_inc(setup_mm, 1)
            pe.wait_ge(setup_lo, 2)
            for h in range(H):
                for k in range(H):
                    last = nc.tensor.matmul(ps_scores[1][:, h * D:(h + 1) * D], wlq_t[:, k, h * P:(h + 1) * P],
                                            wlk_t[:, k, :], start=k == 0, stop=k == H - 1)
            last.then_inc(setup_mm, 1)
            pe.wait_ge(setup_lo, 8)
            pe.wait_ge(ones_set, 2)

            def key_transposes(t):
                s, first_tile = t.b * UNIT // SLAB, t.b * UNIT % SLAB
                if first_tile == 0:
                    pe.wait_ge(slab_in[s], (t.i + (TILES // SLAB // 2 * t.layer + 1)) * 16)
                if t.layer == 0:
                    begins = isinstance(t.u, int) and t.u == 0
                    ends = isinstance(t.u, int) and t.u == UNITS - 1
                    for b in range(UNIT):
                        for h in range(H):
                            nc.tensor.matmul(ps_sum[h], slab[:, s, first_tile + b, h * P:(h + 1) * P], ones_f[:, 0:1],
                                             start=begins and b == 0, stop=ends and b == UNIT - 1,
                                             skip_group_check=True)
                for h in range(H):
                    for b in range(UNIT):
                        rows = slab[:, s, first_tile + b, h * P:(h + 1) * P]
                        last = nc.tensor.transpose(ps_t[t.slot][:, (h * UNIT + b) * P:(h * UNIT + b + 1) * P], rows,
                                                   ident[:])
                last.then_inc(xt_mm, 1)

            def value_product(v):
                s = v.slot
                pe.wait_ge(xt_lo, v.n + 1)
                if v.layer or not isinstance(v.u, int) or v.u >= 2:
                    pe.wait_ge(value_lo, v.n - 1)
                for b in range(UNIT):
                    dst = ps_value[s][:, b * D:(b + 1) * D]
                    last = split_mm(dst, lambda k, h: (x_hi, x_lo)[k][:, s, h, b * P:(b + 1) * P],
                                    lambda k, h: w_v[:, k, h], stop=v.layer == 1)
                    if v.layer == 0:
                        nc.tensor.matmul(dst, ones[:], blv_hi[:], start=False, stop=False)
                        last = nc.tensor.matmul(dst, ones[:], blv_lo[:], start=False, stop=True)
                last.then_inc(value_mm, 1)

            def key_value_unit(t, v):
                if t is not None:
                    key_transposes(t)
                if v is not None:
                    value_product(v)

            def query_transposes(t):
                pe.wait_ge(rows_q_in, t.loads())
                for h in range(H):
                    for par in range(2):
                        last = nc.tensor.transpose(ps_proj[:, (2 * h + par) * P:(2 * h + par + 1) * P],
                                                   rows_q[:, par, h * P:(h + 1) * P], ident[:])
                last.then_inc(rt_mm, 1)

            def query_product(t):
                pe.wait_ge(rt_lo, t.m + 1)
                for half in range(H):
                    last = split_mm(ps_proj[:, half * 2 * P:(half + 1) * 2 * P],
                                    lambda k, h: w_q[:, k, h, half * P:(half + 1) * P],
                                    lambda k, h: r_split[:, k, h])
                last.then_inc(q_mm, 1)

            def edge_values(t):
                pe.wait_ge(q_lo, t.m + 1)
                for par in range(2):
                    last = split_mm(ps_proj[:, par * D:(par + 1) * D],
                                    lambda k, h: r_split[:, k, h, par * P:(par + 1) * P],
                                    lambda k, h: w_ev[:, k, h])
                last.then_inc(edge_mm, 1)

            def scores(t, c):
                dst = ps_scores[c % 2]
                for h in range(H):
                    for k, keys in ((0, keys_hi), (0, keys_lo), (1, keys_hi)):
                        for b in range(CHUNK // BANK):
                            col = c * CHUNK + b * BANK
                            last = nc.tensor.matmul(dst[:, b * BANK:(b + 1) * BANK], q_split[:, k, h, t.par * P:(t.par + 1) * P],
                                                    keys[:, h, col:col + BANK],
                                                    start=h == 0 and k == 0 and keys is keys_hi,
                                                    stop=h == H - 1 and k == 1, skip_group_check=True)
                last.then_inc(scores_mm, 1)

            def prob_transposes(t, g):
                if g % 2 == 0:
                    pe.wait_ge(exped, t.n * CHUNKS + (g // 2 + 1))
                for b in range(GROUP):
                    col = (g * GROUP + b) * P
                    last = nc.tensor.transpose(ps_t[g % 2][:, b * P:(b + 1) * P], probs[:, t.par, col:col + P],
                                               ident[:])
                last.then_inc(pt_mm, 1)

            def values_product(t, g):
                for b in range(GROUP):
                    j, sl = g * GROUP + b, slice(b * P, (b + 1) * P)
                    nc.tensor.matmul(ps_out[:], pt_hi[:, g % RING, sl], values[:, j, :],
                                     start=j == 0, stop=False, skip_group_check=True)
                    last = nc.tensor.matmul(ps_out[:, 0:D], pt_lo[:, g % RING, sl], values[:, j, 0:D],
                                            start=False, stop=j == TILES - 1, skip_group_check=True)
                last.then_inc(pv_mm, 1)

            def step(cur, nxt, far):
                for c in range(CHUNKS):
                    if c == 3:
                        if far is not None and far.par == 0:
                            pe.wait_ge(q_lo, far.m)
                            if cur.layer == 0:
                                pe.wait_ge(edge_set, far.n)
                            query_transposes(far)
                        if cur is not None:
                            prob_transposes(cur, 0)
                            prob_transposes(cur, 1)
                    if nxt is not None:
                        if c == 0:
                            pe.wait_ge(q_lo, nxt.m + 1)
                        if cur is not None or c >= 2 or nxt.layer:
                            pe.wait_ge(masked, nxt.n * CHUNKS + (c - 1))
                        scores(nxt, c)
                if cur is None and nxt.layer == 0:
                    edge_values(nxt)
                if cur is not None:
                    for g in range(GROUPS):
                        pe.wait_ge(pt_lo_set, cur.n * GROUPS + (g + 1))
                        if g + 2 < GROUPS:
                            prob_transposes(cur, g + 2)
                        if g == 0:
                            wait_used(pe, out_read, cur.n)
                        values_product(cur, g)
                        if g == 1 and far is not None and far.par == 0:
                            if far.layer != cur.layer:
                                pe.wait_ge(w_q1_in, 16)
                            query_product(far)
                        if g == 3 and nxt is not None and nxt.par == 0 and nxt.layer == 0:
                            edge_values(nxt)

            first = Tile(0, 0, 0)
            query_transposes(first)
            query_product(first)
            for layer in range(2):
                if layer:
                    pe.wait_ge(w_v1_in, 16)
                units(pe, layer, key_value_unit)
                if layer == 0:
                    pe.wait_ge(mean_step, H)
                    pe.wait_ge(biases_in, 16 * 5)
                    for h in range(H):
                        for k in range(H):
                            last = nc.tensor.matmul(ps_proj[:, h * P:(h + 1) * P], wgk[:, k, h * P:(h + 1) * P],
                                                    x_bar[:, k], start=k == 0, stop=k == H - 1)
                    last.then_inc(global_mm, 1)
                    for k in range(H):
                        last = nc.tensor.matmul(ps_out[:, 0:D], x_bar[:, k], wgv[:, k], start=k == 0, stop=k == H - 1)
                    last.then_inc(global_mm, 1)
                    pe.wait_ge(global_set, 1)
                    for k in range(H):
                        last = nc.tensor.matmul(ps_t[0][:, 0:D], gk[:, k], wgq_t[:, k], start=k == 0, stop=k == H - 1)
                    last.then_inc(global_mm, 1)
                    pe.wait_ge(global_set, 3)
                pe.wait_ge(keys_hi_set, UNITS * (layer + 1))
                pe.wait_ge(keys_lo_set, UNITS * (layer + 1))
                pe.wait_ge(value_lo, UNITS * (layer + 1))
                steps(pe, layer, step)

        @block.scalar
        def _(act):
            def hi(dst, src, **kw):
                return nc.scalar.activation(dst, src, ACT.Copy, **kw)

            act.wait_ge(weights_in[1], 16 * 7)
            hi(w_v[:, 0], raw["Wlv"][:]).then_inc(setup_hi, 1)
            hi(w_ev[:, 0], raw["Wev"][:]).then_inc(setup_hi, 1)
            hi(blv_hi[:], blv[:]).then_inc(setup_hi, 1)
            act.wait_ge(setup_mm, 3)
            hi(wgq_t[:], ps_out[:]).then_inc(setup_hi, 1)
            act.wait_ge(setup_mm, 4)
            hi(w_v1[:, 0], ps_proj[:]).then_inc(setup_hi, 1)
            act.wait_ge(setup_mm, 5)
            hi(w_q1[:, 0], ps_scores[0][:, 0:BANK]).then_inc(setup_hi, 1)
            act.wait_ge(setup_mm, 6)
            hi(w_q[:, 0], ps_scores[1][:, 0:BANK], scale=SCALE).then_inc(setup_hi, 1)

            def unit_values(v, k):
                return values[:, bass.ds(v.u * UNIT, UNIT), k * D:(k + 1) * D]

            def key_value_unit(t, v):
                if t is not None:
                    act.wait_ge(xt_mm, t.n + 1)
                    if t.layer or not isinstance(t.u, int) or t.u >= 2:
                        act.wait_ge(value_mm, t.n - 1)
                    hi(x_hi[:, t.slot], ps_t[t.slot][:]).then_inc(xt_hi, 1)
                    act.wait_ge(xt_hi, t.n + 1)
                    hi(keys_hi[:, :, bass.ds(t.u * (UNIT * P), UNIT * P)], f32(x_hi[:, t.slot])).then_inc(keys_hi_set, 1)
                if v is not None:
                    act.wait_ge(value_mm, v.n + 1)
                    hi(unit_values(v, 0), ps_value[v.slot]).then_inc(value_hi, 1)

            def mask_chunk(t, c):
                if t.layer == 0:
                    if c == 0:
                        act.wait_ge(adj_in[t.par], t.layer_loads())
                    src = adj8[:, t.par * N + c * CHUNK:t.par * N + (c + 1) * CHUNK]
                else:
                    act.wait_ge(adj_t_in[c], t.layer_loads())
                    src = adj8[:].rearrange("p (j two) -> p two j", two=2)[:, t.par, c * CHUNK:(c + 1) * CHUNK]
                nc.scalar.activation(mask[:, c], src, ACT.Copy, scale=-MASKED[t.layer], bias=MASKED[t.layer]
                                     ).then_inc(mask_set, 1)

            def next_mask(t, c):
                act.wait_ge(masked, t.n * CHUNKS + (c + 1 - CHUNKS))
                mask_chunk(t, c)

            def exp_chunk(t, c):
                if c == 0:
                    act.wait_ge(max_set, t.n + 1)
                    wait_used(act, sums_used, t.n - 1)
                    if t.layer == 0:
                        nc.scalar.activation(ge_exp[:, t.par], row_max[:, t.par, 4:6], ACT.Exp,
                                             bias=neg_max[:, t.par:t.par + 1], accum_out=sums[:, t.par, 4:5])
                chunk = probs[:, t.par, c * CHUNK:(c + 1) * CHUNK]
                nc.scalar.activation(chunk, chunk, ACT.Exp, bias=neg_max[:, t.par:t.par + 1],
                                     accum_out=sums[:, t.par, c:c + 1]).then_inc(exped, 1)

            def query_rows_hi(t):
                act.wait_ge(rt_mm, t.m + 1)
                hi(r_split[:, 0], ps_proj[:]).then_inc(rt_hi, 1)

            def query_hi(t):
                act.wait_ge(q_mm, t.m + 1)
                hi(q_split[:, 0], ps_proj[:]).then_inc(q_hi, 1)

            def prob_hi(t, g):
                act.wait_ge(pt_mm, t.n * GROUPS + (g + 1))
                if g < RING:
                    wait_used(act, out_read, t.n)
                else:
                    act.wait_ge(pv_mm, t.n * GROUPS + (g + 1 - RING))
                hi(pt_hi[:, g % RING], ps_t[g % 2][:]).then_inc(pt_hi_set, 1)

            def step(cur, nxt, far):
                queries = far is not None and far.par == 0
                masks = far is not None and (cur is None or far.layer == cur.layer)
                if cur is not None:
                    exp_chunk(cur, 2)
                    exp_chunk(cur, 3)
                if masks:
                    next_mask(far, 0)
                    next_mask(far, 1)
                if queries:
                    query_rows_hi(far)
                if cur is not None:
                    prob_hi(cur, 0)
                    prob_hi(cur, 1)
                if masks:
                    next_mask(far, 2)
                if cur is not None:
                    prob_hi(cur, 2)
                if masks:
                    next_mask(far, 3)
                if cur is not None:
                    prob_hi(cur, 3)
                if nxt is not None:
                    exp_chunk(nxt, 0)
                if queries:
                    query_hi(far)
                if cur is not None:
                    prob_hi(cur, 4)
                if nxt is not None:
                    exp_chunk(nxt, 1)
                if cur is not None:
                    for g in range(5, GROUPS):
                        prob_hi(cur, g)
                if cur is not None and nxt is None and cur.layer == 0:
                    for c in range(CHUNKS):
                        next_mask(Tile(1, 0, 0), c)

            first = Tile(0, 0, 0)
            query_rows_hi(first)
            query_hi(first)
            for layer in range(2):
                units(act, layer, key_value_unit)
                if layer == 0:
                    for c in range(CHUNKS):
                        mask_chunk(first, c)
                steps(act, layer, step)

        @block.vector
        def _(dve):
            def lo(dst, src, hi_half):
                return nc.vector.tensor_tensor(dst, src, f32(hi_half), ALU.subtract)

            dve.wait_ge(setup_mm, 1)
            nc.vector.tensor_copy(wlq_t[:], ps_t[0][:]).then_inc(setup_lo, 1)
            dve.wait_ge(setup_mm, 2)
            nc.vector.tensor_copy(wlk_t[:], ps_t[1][:]).then_inc(setup_lo, 1)
            dve.wait_ge(setup_hi, 3)
            lo(w_v[:, 1], raw["Wlv"][:], w_v[:, 0]).then_inc(setup_lo, 1)
            lo(w_ev[:, 1], raw["Wev"][:], w_ev[:, 0]).then_inc(setup_lo, 1)
            lo(blv_lo[:], blv[:], blv_hi[:]).then_inc(setup_lo, 1)
            dve.wait_ge(setup_hi, 5)
            lo(w_v1[:, 1], ps_proj[:], w_v1[:, 0]).then_inc(setup_lo, 1)
            dve.wait_ge(setup_hi, 6)
            lo(w_q1[:, 1], ps_scores[0][:, 0:BANK], w_q1[:, 0]).then_inc(setup_lo, 1)
            dve.wait_ge(setup_hi, 7)
            nc.vector.scalar_tensor_tensor(out=w_q[:, 1], in0=ps_scores[1][:, 0:BANK], scalar=SCALE,
                                           in1=f32(w_q[:, 0]), op0=ALU.mult, op1=ALU.subtract).then_inc(setup_lo, 1)

            def unit_values(v, k):
                return values[:, bass.ds(v.u * UNIT, UNIT), k * D:(k + 1) * D]

            def key_value_unit(t, v):
                if t is not None:
                    dve.wait_ge(xt_hi, t.n + 1)
                    if t.layer or not isinstance(t.u, int) or t.u >= 2:
                        dve.wait_ge(keys_lo_set, t.n - 1)
                    lo(x_lo[:, t.slot], ps_t[t.slot][:], x_hi[:, t.slot]).then_inc(xt_lo, 1)
                if v is not None:
                    dve.wait_ge(value_hi, v.n + 1)
                    lo(unit_values(v, 1), ps_value[v.slot], unit_values(v, 0)).then_inc(value_lo, 1)

            def global_terms():
                dve.wait_ge(xt_mm, UNITS)
                for h in range(H):
                    nc.vector.tensor_copy(x_total[:, h:h + 1], ps_sum[h]).then_inc(sums_read, 1)
                dve.wait_ge(sums_read, H)
                dve.wait_ge(ones_set, 1)
                for h in range(H):
                    nc.vector.tensor_scalar(x_bar[:, h], ones_f[:], x_total[:, h:h + 1], 1.0 / N, ALU.mult, ALU.mult
                                            ).then_inc(mean_step, 1)
                dve.wait_ge(global_mm, 1)
                nc.vector.tensor_copy(gk[:], ps_proj[:, 0:D]).then_inc(global_set, 1)
                dve.wait_ge(biases_in, 16 * 5)
                dve.wait_ge(global_mm, 2)
                nc.vector.tensor_tensor(gv_bc[:], ps_out[:, 0:D], gv_bc[:], ALU.add).then_inc(global_set, 1)
                dve.wait_ge(global_mm, 3)
                nc.vector.tensor_scalar(u_bc[:], ps_t[0][:, 0:D], SCALE, None, ALU.mult).then_inc(global_set, 1)
                dve.wait_ge(global_set, 3)

            def row_dots(t):
                dve.wait_ge(rows_q_in, t.loads())
                wait_used(dve, exped, t.n * CHUNKS + (1 - 2 * CHUNKS))
                for k, vec, dot in ((0, u_bc, global_dot), (1, wes_bc, edge_dot)):
                    nc.vector.tensor_tensor_reduce(out=dot_out[:], in0=rows_q[:, t.par], in1=vec[:], scale=1.0,
                                                   scalar=0.0, op0=ALU.mult, op1=ALU.add,
                                                   accum_out=row_max[:, t.par, 4 + k:5 + k]).then_inc(dot, 1)
                    dve.wait_ge(dot, t.n + 1)

            def query_rows_lo(t):
                dve.wait_ge(rt_hi, t.m + 1)
                lo(r_split[:, 1], ps_proj[:], r_split[:, 0]).then_inc(rt_lo, 1)

            def query_lo(t):
                dve.wait_ge(q_hi, t.m + 1)
                lo(q_split[:, 1], ps_proj[:], q_split[:, 0]).then_inc(q_lo, 1)

            def edge_rows(t):
                dve.wait_ge(edge_mm, t.m + 1)
                nc.vector.tensor_tensor(edge_v[:, t.par], ps_proj[:, t.par * D:(t.par + 1) * D], bev_bc[:], ALU.add
                                        ).then_inc(edge_set, 1)

            def mask_scores(t, c):
                count = dve.compute_val(t.n * CHUNKS + (c + 1))
                dve.wait_ge(keys_lo_set, UNITS * (t.layer + 1))
                dve.wait_ge(mask_set, count)
                dve.wait_ge(scores_mm, count)
                nc.vector.tensor_tensor_reduce(out=probs[:, t.par, c * CHUNK:(c + 1) * CHUNK], in0=ps_scores[c % 2][:],
                                               in1=mask[:, c], scale=1.0, scalar=-3e38, op0=ALU.add, op1=ALU.max,
                                               accum_out=row_max[:, t.par, c:c + 1]).then_inc(masked, 1)

            def set_max(t):
                dve.wait_ge(masked, t.n * CHUNKS + CHUNKS)
                wait_used(dve, exped, t.n * CHUNKS - CHUNKS)
                nc.vector.tensor_reduce(neg_max[:, t.par:t.par + 1], row_max[:, t.par, 0:6 if t.layer == 0 else 5],
                                        AX.X, ALU.max, negate=True).then_inc(max_set, 1)

            def prob_lo(t, g):
                dve.wait_ge(pt_hi_set, t.n * GROUPS + (g + 1))
                lo(pt_lo[:, g % RING], ps_t[g % 2][:], pt_hi[:, g % RING]).then_inc(pt_lo_set, 1)

            def epilogue(t):
                if t.layer == 0:
                    before = t.n * EPI_STEPS[0]
                else:
                    before = t.n * EPI_STEPS[1] + TILES * (EPI_STEPS[0] - EPI_STEPS[1])
                done = [0]

                def then(ins):
                    done[0] += 1
                    ins.then_inc(epi_step, 1)
                    dve.wait_ge(epi_step, before + done[0])

                p = t.par
                d, r = den[:, p:p + 1], rden[:, 0:1]
                dve.wait_ge(exped, t.n * CHUNKS + CHUNKS)
                if t.layer == 0:
                    then(nc.vector.reduce_sum(d, sums[:, p, 0:5], AX.X))
                    then(nc.vector.reciprocal(r, d))
                    nc.vector.tensor_scalar(ge_w[:], ge_exp[:, p], r, None, ALU.mult).then_inc(sums_used, 1)
                    dve.wait_ge(sums_used, t.n + 1)
                    then(nc.vector.tensor_scalar(y_tmp[:], gv_bc[:], ge_w[:, 0:1], None, ALU.mult))
                    dve.wait_ge(edge_set, t.n + 1)
                    then(nc.vector.scalar_tensor_tensor(out=y_tmp[:], in0=edge_v[:, p], scalar=ge_w[:, 1:2],
                                                        in1=y_tmp[:], op0=ALU.mult, op1=ALU.add))
                    add = y_tmp[:]
                    dve.wait_ge(rows_res_in[0][p], t.layer_loads(2))
                else:
                    nc.vector.reduce_sum(d, sums[:, p, 0:4], AX.X).then_inc(sums_used, 1)
                    dve.wait_ge(sums_used, t.n + 1)
                    then(nc.vector.tensor_scalar(d, d, TINY, None, ALU.max))
                    then(nc.vector.reciprocal(r, d))
                    add = rows_max[:, p]
                    dve.wait_ge(rows_res_in[1][p], t.layer_loads())
                    dve.wait_ge(normed, t.n - 1)
                dve.wait_ge(pv_mm, t.n * GROUPS + GROUPS)
                then(nc.vector.scalar_tensor_tensor(out=y_tmp[:], in0=ps_out[:, 0:D], scalar=r, in1=add,
                                                    op0=ALU.mult, op1=ALU.add))
                out_t = y_tmp[:] if t.layer == 0 else rows_res[:, p]
                nc.vector.scalar_tensor_tensor(out=out_t, in0=ps_out[:, D:2 * D], scalar=r, in1=y_tmp[:],
                                               op0=ALU.mult, op1=ALU.add).then_inc(out_read, 1)
                dve.wait_ge(out_read, t.n + 1)
                if t.layer == 0:
                    then(nc.vector.tensor_tensor(y_tmp[:], y_tmp[:], rows_max[:, p], ALU.max))
                    then(nc.vector.tensor_tensor(rows_res[:, p], y_tmp[:], rows_res[:, p], ALU.add))
                nc.vector.bn_stats(stats[:], rows_res[:, p])
                dve.drain()
                nc.vector.bn_aggr(mean_var[:, p], stats[:]).then_inc(stats_set, 1)
                assert done[0] == EPI_STEPS[t.layer]

            def step(cur, nxt, far):
                queries = far is not None and far.par == 0
                edges = nxt is not None and nxt.par == 0 and nxt.layer == 0
                if nxt is not None:
                    mask_scores(nxt, 0)
                    mask_scores(nxt, 1)
                    mask_scores(nxt, 2)
                if queries:
                    query_rows_lo(far)
                if cur is not None:
                    prob_lo(cur, 0)
                    prob_lo(cur, 1)
                if nxt is not None:
                    mask_scores(nxt, 3)
                    set_max(nxt)
                if far is not None and far.layer == 0:
                    row_dots(far)
                if cur is None and edges:
                    edge_rows(nxt)
                    edge_rows(nxt.after(1))
                if cur is not None:
                    for g in range(2, GROUPS):
                        prob_lo(cur, g)
                        if g == 3 and queries:
                            query_lo(far)
                        if g == 5 and edges:
                            edge_rows(nxt)
                    epilogue(cur)
                    if edges:
                        edge_rows(nxt.after(1))

            first = Tile(0, 0, 0)
            query_rows_lo(first)
            query_lo(first)
            for layer in range(2):
                units(dve, layer, key_value_unit)
                if layer == 0:
                    global_terms()
                    row_dots(first)
                    dve.wait_ge(w1_out, 32)
                else:
                    for par in range(2):
                        nc.vector.memset(row_max[:, par, 4:5], FLOOR).then_inc(floor_set, 1)
                    dve.wait_ge(floor_set, 2)
                steps(dve, layer, step)


_INS = ['x', 'adj', 'L0_gnn_masked_x', 'L0_gnn_Wlq', 'L0_gnn_Wlk', 'L0_gnn_Wlv', 'L0_gnn_blv', 'L0_gnn_Wgq',
        'L0_gnn_Wgk', 'L0_gnn_Wgv', 'L0_gnn_bgv', 'L0_gnn_Wes', 'L0_gnn_Wev', 'L0_gnn_bev', 'L1_gnn_Wq',
        'L1_gnn_Wk', 'L1_gnn_Wv']


def kernel(**inputs):
    import numpy as _np
    import concourse.bacc as _bacc
    from concourse import mybir as _mybir
    from concourse.bass_utils import run_bass_kernel_spmd as _run

    nc = _bacc.Bacc("TRN2", target_bir_lowering=False, num_devices=1, dynamic_dma_scratch_size=1024)
    arrays, args = {}, {}
    for name in _INS:
        arr = _np.ascontiguousarray(inputs[name])
        arrays[f"in_{name}_dram"] = arr
        args[name] = nc.dram_tensor(f"in_{name}_dram", arr.shape, _mybir.dt.from_np(arr.dtype),
                                    kind="ExternalInput").ap()
    out = nc.dram_tensor("out_dram", (N, D), _mybir.dt.float32, kind="ExternalOutput").ap()
    adj_resnorm(nc, args, out)
    r = _run(nc, [arrays], core_ids=[0])
    return r.results[0]["out_dram"]
```

```python
from contextlib import ExitStack

import concourse.bass as bass
from concourse import mybir

F32 = mybir.dt.float32
F32R = mybir.dt.float32r
BF16 = mybir.dt.bfloat16
U8 = mybir.dt.uint8
U16 = mybir.dt.uint16
ALU = mybir.AluOpType
ACT = mybir.ActivationFunctionType
AX = mybir.AxisListType

P = 128
N = 4096
D = 256
H = D // P
TILES = N // P
PAIRS = TILES // 2
CHUNK = 1024
CHUNKS = N // CHUNK
BANK = 512
GROUP = 4
GROUPS = TILES // GROUP
RING = 3
SLAB = 4
UNIT = 2
UNITS = TILES // UNIT
BODY = 2 * SLAB // UNIT
BIAS_ROWS = 33
SCALE = float(D) ** -0.5
EPS = 1e-5
MASKED = (-1e9, -1e30)
FLOOR = -1e29
TINY = 1e-30
EPI_STEPS = (7, 3)


class Tile:

    def __init__(self, layer, pair, par):
        self.layer, self.pair, self.par = layer, pair, par
        self.n = pair * 2 + (TILES * layer + par)
        self.m = pair + PAIRS * layer

    def after(self, k):
        q = self.par + k
        return Tile(self.layer, self.pair + q // 2, q % 2)

    def loads(self, dmas=1):
        return (self.m + 1) * (16 * dmas)

    def layer_loads(self, dmas=1):
        return (self.pair + 1) * (16 * dmas)


class Unit:

    def __init__(self, layer, i, b):
        self.layer, self.i, self.b, self.slot = layer, i, b, b % 2
        self.u = i * BODY + b
        self.n = i * BODY + (UNITS * layer + b)

    def before(self):
        return Unit(self.layer, self.i - (self.b == 0), (self.b - 1) % BODY)

    def after(self):
        return Unit(self.layer, self.i + (self.b + 1) // BODY, (self.b + 1) % BODY)


def loop(eng, layer, count, body):
    if layer == 0:
        body(0)
    with eng.Fori(1 - layer, count) as i:
        body(i)


def wait_used(eng, sem, value):
    if not isinstance(value, int) or value > 0:
        eng.wait_ge(sem, value)


def steps(eng, layer, step):
    first = Tile(layer, 0, 0)
    step(None, first, first.after(1))

    def body(pair):
        for par in range(2):
            cur = Tile(layer, pair, par)
            step(cur, cur.after(1), cur.after(2))

    loop(eng, layer, PAIRS - 1, body)
    cur = Tile(layer, PAIRS - 1, 0)
    step(cur, cur.after(1), None)
    step(cur.after(1), None, None)


def units(eng, layer, step, after_body=None):
    def body(i):
        for b in range(BODY):
            u = Unit(layer, i, b)
            step(u.after(), u, None if isinstance(i, int) and u.u == 0 else u.before())

    body(0)
    if after_body is not None:
        after_body()
    with eng.Fori(1, UNITS // BODY - 1) as i:
        body(i)
    for b in range(BODY):
        u = Unit(layer, UNITS // BODY - 1, b)
        step(u.after() if b < BODY - 1 else None, u, u.before())
    step(None, None, u)


def adj_resnorm(nc, a, out):
    with ExitStack() as ctx:
        def sem(name):
            return ctx.enter_context(nc.semaphore(name))

        size = {F32: 4, F32R: 4, BF16: 2, U8: 1, U16: 2}
        top = [-(-nc.sbuf_base // 32) * 32]

        def place(name, shape, dt, at=None):
            nbytes = size[dt]
            for d in shape[1:]:
                nbytes *= d
            where = top if at is None else at
            t = nc.alloc_sbuf_tensor_at(name, shape, dt, offset=where[0])
            where[0] += -(-nbytes // 32) * 32
            return t

        keys_hi = place("keys_hi", [P, H, N], F32R)
        keys_lo = place("keys_lo", [P, H, N], F32R)
        values_at = list(top)
        values = place("values", [P, TILES, 2 * D], F32R)
        probs_at = list(top)
        probs = place("probs", [P, 2, N], F32)
        ring_at = list(top)
        pt_hi = place("pt_hi", [P, RING, BANK], F32R)
        pt_lo = place("pt_lo", [P, RING, BANK], F32R)
        adj8 = place("adj8", [P, 2 * N], U8)
        mask = place("mask", [P, CHUNKS, CHUNK], BF16)
        q_split = place("q_split", [P, 2, H, 2 * P], F32R)
        r_split = place("r_split", [P, 2, H, 2 * P], F32R)
        rows_q = place("rows_q", [P, 2, D], F32)
        rows_max = place("rows_max", [P, 2, D], F32)
        rows_res = place("rows_res", [P, 2, D], F32)
        edge_v = place("edge_v", [P, 2, D], F32)
        out_rows = place("out_rows", [P, 2, D], F32)
        y_tmp = place("y_tmp", [P, D], F32)
        dot_out = place("dot_out", [P, D], F32)
        w_ev = place("w_ev", [P, 2, H, D], F32R)
        w_q = place("w_q", [P, 2, H, D], F32R)
        ident = place("ident", [P, P], F32)
        u_bc = place("u_bc", [P, D], F32)
        wes_bc = place("wes_bc", [P, D], F32)
        gv_bc = place("gv_bc", [P, D], F32)
        bev_bc = place("bev_bc", [P, D], F32)
        row_max = place("row_max", [P, 2, 6], F32)
        neg_max = place("neg_max", [P, 2], F32)
        sums = place("sums", [P, 2, 5], F32)
        ge_exp = place("ge_exp", [P, 2, 2], F32)
        ge_w = place("ge_w", [P, 2], F32)
        den = place("den", [P, 2], F32)
        rden = place("rden", [P, 1], F32)
        stats = place("stats", [P, 6], F32)
        mean_var = place("mean_var", [P, 2, 2], F32)
        var_eps = place("var_eps", [P, 1], F32)
        rstd = place("rstd", [P, 1], F32)
        minus_half = place("minus_half", [P, 1], F32)
        eps = place("eps", [P, 1], F32)
        w_v = place("w_v", [P, 2, H, D], F32R, probs_at)
        slab = place("slab", [P, 2, SLAB, D], F32, probs_at)
        x_hi = place("x_hi", [P, 2, H, UNIT * P], F32R, probs_at)
        x_lo = place("x_lo", [P, 2, H, UNIT * P], F32R, probs_at)
        w_v1 = place("w_v1", [P, 2, H, D], F32R, probs_at)
        w_q1 = place("w_q1", [P, 2, H, D], F32R, probs_at)
        blv = place("blv", [BIAS_ROWS, D], F32, probs_at)
        blv_split = place("blv_split", [BIAS_ROWS, D], F32R, probs_at)
        blv_rows = place("blv_rows", [BIAS_ROWS, P], F32R, probs_at)
        x_sums = place("x_sums", [P, UNITS, H], F32, probs_at)
        wgk = place("wgk", [P, H, D], F32, ring_at)
        wgv = place("wgv", [P, H, D], F32, ring_at)
        wgq_t = place("wgq_t", [P, H, D], F32, ring_at)
        x_bar = place("x_bar", [P, H, P], F32, ring_at)
        gk = place("gk", [P, H, P], F32, ring_at)
        x_total = place("x_total", [P, H], F32, ring_at)
        ones_f = place("ones_f", [P, P], F32, ring_at)
        raw = {w: place(f"raw_{w}", [P, H, D], F32, values_at)
               for w in ("Wlq", "Wlk", "Wgq", "Wlv", "Wev", "Wq", "Wk", "Wv")}
        wlq_t = place("wlq_t", [P, H, D], F32, values_at)
        wlk_t = place("wlk_t", [P, H, D], F32, values_at)

        def psum(name, cols):
            return ctx.enter_context(nc.psum_tensor(name, [P, cols], F32))

        ps_scores = [psum(f"ps_scores{i}", CHUNK) for i in range(2)]
        ps_t = [psum(f"ps_t{i}", BANK) for i in range(2)]
        ps_out = psum("ps_out", BANK)
        ps_proj = psum("ps_proj", BANK)
        ps_value = [ps_scores[b // 2][:, b % 2 * BANK:(b % 2 + 1) * BANK] for b in range(BODY)]

        x1 = nc.dram_tensor("x1_rows", (N, D), F32).ap()
        w1_kept = nc.dram_tensor("w1_kept", (2, P, 2 * H * D), F32).ap()
        x1_pairs = x1.rearrange("(n two) d -> n (two d)", two=2)
        out_pairs = out.rearrange("(n two) d -> n (two d)", two=2)
        adj16 = a["adj"].bitcast(U16)
        masked_x, x = a["L0_gnn_masked_x"], a["x"]

        weights_in = [sem(f"weights_in{i}") for i in range(3)]
        biases_in = sem("biases_in")
        slab_in = [sem(f"slab_in{i}") for i in range(2)]
        rows_q_in = sem("rows_q_in")
        rows_res_in = [[sem(f"rows_res_in{l}{i}") for i in range(2)] for l in range(2)]
        adj_in = [sem(f"adj_in{i}") for i in range(2)]
        adj_t_in = [sem(f"adj_t_in{c}") for c in range(CHUNKS)]
        stored = [sem(f"stored{i}") for i in range(2)]
        const_set = sem("const_set")
        ident_set = sem("ident_set")
        ones_set = sem("ones_set")
        floor_set = sem("floor_set")
        w1_out = sem("w1_out")
        w_v1_in = sem("w_v1_in")
        w_q1_in = sem("w_q1_in")
        setup_mm = sem("setup_mm")
        setup_hi = sem("setup_hi")
        setup_lo = sem("setup_lo")
        xt_mm = sem("xt_mm")
        xt_hi = sem("xt_hi")
        xt_lo = sem("xt_lo")
        keys_hi_set = sem("keys_hi_set")
        keys_lo_set = sem("keys_lo_set")
        value_mm = sem("value_mm")
        value_hi = sem("value_hi")
        value_lo = sem("value_lo")
        x_summed = sem("x_summed")
        mean_step = sem("mean_step")
        global_mm = sem("global_mm")
        global_set = sem("global_set")
        rt_mm = sem("rt_mm")
        rt_hi = sem("rt_hi")
        rt_lo = sem("rt_lo")
        q_mm = sem("q_mm")
        q_hi = sem("q_hi")
        q_lo = sem("q_lo")
        edge_mm = sem("edge_mm")
        edge_set = sem("edge_set")
        global_dot = sem("global_dot")
        edge_dot = sem("edge_dot")
        scores_mm = sem("scores_mm")
        mask_set = sem("mask_set")
        masked = sem("masked")
        max_set = sem("max_set")
        exped = sem("exped")
        pt_mm = sem("pt_mm")
        pt_hi_set = sem("pt_hi_set")
        pt_lo_set = sem("pt_lo_set")
        pv_mm = sem("pv_mm")
        sums_used = sem("sums_used")
        out_read = sem("out_read")
        epi_step = sem("epi_step")
        stats_set = sem("stats_set")
        var_step = sem("var_step")
        normed = sem("normed")

        def f32(t):
            return t.bitcast(F32)

        def query_halves(t, k):
            if t.layer == 0:
                return q_split[:, k], ps_proj[:]
            return (q_split[:, k].rearrange("p f (two q) -> p f two q", two=2),
                    ps_proj[:].rearrange("p (f q two) -> p f two q", f=H, two=2))

        block = ctx.enter_context(nc.Block())

        @block.sync
        def _(sp):
            def w_rows(w):
                return w.rearrange("(h p) d -> p h d", p=P)

            def load_rows_q(t):
                rows = masked_x[bass.ds(t.pair * (2 * P), 2 * P), :].rearrange("(t p) d -> p t d", p=P)
                sp.dma_start(rows_q[:], rows).then_inc(rows_q_in, 16)

            def load_weights(k, names):
                for w in names:
                    sp.dma_start(raw[w[7:]][:], w_rows(a[w])).then_inc(weights_in[k], 16)

            load_weights(0, ("L0_gnn_Wlq", "L0_gnn_Wlk"))
            load_weights(1, ("L1_gnn_Wq", "L1_gnn_Wk"))
            load_rows_q(Tile(0, 0, 0))
            load_weights(2, ("L0_gnn_Wgq", "L1_gnn_Wv", "L0_gnn_Wlv", "L0_gnn_Wev"))
            row = a["L0_gnn_blv"].rearrange("(o d) -> o d", o=1)
            sp.dma_start(blv[:], row.to_broadcast([BIAS_ROWS, D])).then_inc(weights_in[2], 16)

            def load_slabs(layer, rows, end, start=0):
                view = rows.rearrange("(g s p) d -> g p s d", s=SLAB, p=P)
                for g in range(start, end):
                    if g >= 2:
                        sp.wait_ge(xt_mm, UNITS * layer + SLAB // UNIT * (g - 1))
                    if layer == 1:
                        for par in range(2):
                            sp.wait_ge(stored[par], 16 * (SLAB // 2) * (g + 1))
                    sp.dma_start(slab[:, g % 2], view[g]).then_inc(slab_in[g % 2], 16)

            def load_rows_res(t):
                s = rows_res_in[t.layer][t.par]
                if t.layer == 0:
                    sp.dma_start(rows_max[:, t.par], masked_x[bass.ds(t.n * P, P), :]).then_inc(s, 16)
                    sp.dma_start(rows_res[:, t.par], x[bass.ds(t.n * P, P), :]).then_inc(s, 16)
                else:
                    sp.dma_start(rows_max[:, t.par], x1_pairs[bass.ds(t.pair * P, P), t.par * D:(t.par + 1) * D]
                                 ).then_inc(s, 16)

            def load_adj(t):
                sp.dma_start(adj8[:, t.par * N:(t.par + 1) * N], a["adj"][bass.ds(t.n * P, P), :]
                             ).then_inc(adj_in[t.par], 16)

            def load_adj_t(t, c):
                sp.dma_start_transpose(adj8.bitcast(U16)[:, c * CHUNK:(c + 1) * CHUNK],
                                       adj16[c * CHUNK:(c + 1) * CHUNK, bass.ds(t.pair * P, P)]
                                       ).then_inc(adj_t_in[c], 16)

            def step(cur, nxt, far):
                if far is not None:
                    if far.layer == 0 and far.par == 0:
                        pairs, tiles = sp.compute_val(far.m), sp.compute_val(far.n)
                        sp.wait_ge(rt_mm, pairs)
                        sp.wait_ge(global_dot, tiles)
                        sp.wait_ge(edge_dot, tiles)
                        load_rows_q(far)
                    if far.layer == 0:
                        if cur is not None:
                            sp.wait_ge(mask_set, far.n * CHUNKS - CHUNKS)
                        load_adj(far)
                    elif far.par == 0:
                        sp.wait_ge(mask_set, far.n * CHUNKS)
                        for c in range(CHUNKS):
                            load_adj_t(far, c)
                if nxt is not None and cur is not None:
                    wait_used(sp, normed, nxt.n - 1)
                    load_rows_res(nxt)
                if nxt is None and cur.layer == 0:
                    sp.wait_ge(mask_set, CHUNKS * TILES)
                    for c in range(CHUNKS):
                        load_adj_t(Tile(1, 0, 0), c)
                    sp.wait_ge(w1_out, 32)
                    sp.wait_ge(q_mm, PAIRS)
                    sp.dma_start(f32(w_q[:]).rearrange(flat), w1_kept[1]).then_inc(w_q1_in, 16)

            flat = "p k h d -> p (k h d)"
            first = Tile(0, 0, 0)
            load_slabs(0, x, 2)
            sp.dma_start(wgk[:], w_rows(a["L0_gnn_Wgk"])).then_inc(biases_in, 16)
            sp.dma_start(wgv[:], w_rows(a["L0_gnn_Wgv"])).then_inc(biases_in, 16)
            for t, name in ((gv_bc, "bgv"), (bev_bc, "bev")):
                row = a["L0_gnn_" + name].rearrange("(o d) -> o d", o=1)
                sp.dma_start(t[:], row.to_broadcast([P, D])).then_inc(biases_in, 16)
            sp.dma_start(wes_bc[:], a["L0_gnn_Wes"].rearrange("d o -> o d").to_broadcast([P, D])).then_inc(biases_in, 16)
            load_slabs(0, x, 4, 2)
            sp.wait_ge(setup_lo, 8)
            sp.dma_start(w1_kept[0], f32(w_v1[:]).rearrange(flat)).then_inc(w1_out, 16)
            sp.dma_start(w1_kept[1], f32(w_q1[:]).rearrange(flat)).then_inc(w1_out, 16)
            load_slabs(0, x, TILES // SLAB, 4)
            load_rows_res(first)
            load_adj(first)
            steps(sp, 0, step)

            first = Tile(1, 0, 0)
            sp.wait_ge(pt_mm, (TILES - 1) * GROUPS)
            sp.dma_start(f32(w_v[:]).rearrange(flat), w1_kept[0]).then_inc(w_v1_in, 16)
            load_slabs(1, x1, TILES // SLAB)
            load_rows_res(first)
            steps(sp, 1, step)

        @block.gpsimd
        def _(pool):
            nc.gpsimd.memset(ident[:], 0.0).then_inc(const_set, 1)
            pool.wait_ge(const_set, 1)
            nc.gpsimd.affine_select(out=ident[:], in_=ident[:], compare_op=ALU.not_equal, fill=1.0, base=0,
                                    pattern=[[-1, P]], channel_multiplier=1).then_inc(ident_set, 1)
            nc.gpsimd.memset(ones_f[:], 1.0).then_inc(ones_set, 1)
            nc.gpsimd.memset(f32(blv_rows[:]), 0.0).then_inc(const_set, 1)
            pool.wait_ge(const_set, 2)
            for row in (0, BIAS_ROWS - 1):
                nc.gpsimd.memset(f32(blv_rows[row:row + 1]), 1.0).then_inc(ones_set, 1)
            pool.wait_ge(ones_set, 3)
            nc.gpsimd.memset(minus_half[:], -0.5).then_inc(const_set, 1)
            nc.gpsimd.memset(eps[:], EPS).then_inc(const_set, 1)
            pool.wait_ge(const_set, 4)

            def norm(t):
                pool.wait_ge(stats_set, t.n + 1)
                nc.gpsimd.tensor_tensor(var_eps[:], mean_var[:, t.par, 1:2], eps[:], ALU.add).then_inc(var_step, 1)
                wait_used(pool, stored[t.par], t.loads() - 16)
                pool.wait_ge(var_step, t.n + 1)
                nc.gpsimd.tensor_tensor(rstd[:], var_eps[:], minus_half[:], ALU.pow)
                pool.drain()
                nc.gpsimd.tensor_scalar(out_rows[:, t.par], rows_res[:, t.par], mean_var[:, t.par, 0:1], rstd[:],
                                        ALU.subtract, ALU.mult).then_inc(normed, 1)
                pool.wait_ge(normed, t.n + 1)
                if t.layer == 0:
                    to = x1[bass.ds(t.n * P, P), :]
                else:
                    to = out_pairs[bass.ds(t.pair * P, P), t.par * D:(t.par + 1) * D]
                nc.gpsimd.dma_start(to, out_rows[:, t.par]).then_inc(stored[t.par], 16)

            def step(cur, nxt, far):
                if cur is not None:
                    norm(cur)

            for layer in range(2):
                def keep_lo(t, *_):
                    if t is not None:
                        pool.wait_ge(xt_lo, t.n + 1)
                        nc.gpsimd.tensor_copy(keys_lo[:, :, bass.ds(t.u * (UNIT * P), UNIT * P)], f32(x_lo[:, t.slot])
                                              ).then_inc(keys_lo_set, 1)

                if layer == 0:
                    keep_lo(Unit(0, 0, 0), None, None)
                    units(pool, 0, keep_lo)
                steps(pool, layer, step)
            for par in range(2):
                pool.wait_ge(stored[par], 2 * 16 * PAIRS)

        @block.tensor
        def _(pe):
            def split_mm(dst, lhs, rhs, start=True, stop=True):
                terms = [(h, i, j) for h in range(H) for i, j in ((0, 0), (0, 1), (1, 0))]
                for n, (h, i, j) in enumerate(terms):
                    last = nc.tensor.matmul(dst, lhs(i, h), rhs(j, h), start=start and n == 0,
                                            stop=stop and n == len(terms) - 1)
                return last

            def transpose_w(dst, w):
                for h in range(H):
                    for k in range(H):
                        last = nc.tensor.transpose(dst[:, h * D + k * P:h * D + k * P + P],
                                                   w[:, k, h * P:(h + 1) * P], ident[:])
                return last

            def weight_product(dst, w, v):
                for h in range(H):
                    for k in range(H):
                        last = nc.tensor.matmul(dst[:, h * D:(h + 1) * D], w[:, k, h * P:(h + 1) * P], v[:, k, :],
                                                start=k == 0, stop=k == H - 1)
                return last

            def key_transposes(t):
                s, first_tile = t.b * UNIT // SLAB, t.b * UNIT % SLAB
                if first_tile == 0:
                    pe.wait_ge(slab_in[s], (t.i + (TILES // SLAB // 2 * t.layer + 1)) * 16)
                if t.layer == 0 and (not isinstance(t.u, int) or t.u >= 2):
                    pe.wait_ge(x_summed, t.n - 1)
                for h in range(H):
                    for b in range(UNIT):
                        rows = slab[:, s, first_tile + b, h * P:(h + 1) * P]
                        last = nc.tensor.transpose(ps_t[t.slot][:, (h * UNIT + b) * P:(h * UNIT + b + 1) * P], rows,
                                                   ident[:])
                last.then_inc(xt_mm, 1)

            def value_product(v):
                pe.wait_ge(xt_lo, v.n + 1)
                if v.layer or not isinstance(v.u, int) or v.u >= BODY:
                    pe.wait_ge(value_lo, v.n + (1 - BODY))
                if v.layer == 0 and isinstance(v.u, int) and v.u == 1:
                    pe.wait_ge(setup_lo, 8)
                for b in range(UNIT):
                    dst = ps_value[v.b][:, b * D:(b + 1) * D]
                    last = split_mm(dst, lambda k, h: (x_hi, x_lo)[k][:, v.slot, h, b * P:(b + 1) * P],
                                    lambda k, h: w_v[:, k, h], stop=v.layer == 1)
                    if v.layer == 0:
                        last = nc.tensor.matmul(dst, blv_rows[:], blv_split[:], start=False, stop=True)
                last.then_inc(value_mm, 1)

            def key_value_unit(t, v, _):
                if t is not None:
                    key_transposes(t)
                if v is not None:
                    value_product(v)

            def query_transposes(t):
                pe.wait_ge(rows_q_in, t.loads())
                for h in range(H):
                    for par in range(2):
                        last = nc.tensor.transpose(ps_proj[:, (2 * h + par) * P:(2 * h + par + 1) * P],
                                                   rows_q[:, par, h * P:(h + 1) * P], ident[:])
                last.then_inc(rt_mm, 1)

            def query_product(t):
                if t.layer == 0:
                    pe.wait_ge(rt_lo, t.m + 1)
                for half in range(H):
                    if t.layer == 0:
                        def rows(k, h):
                            return r_split[:, k, h]
                    else:
                        def rows(k, h):
                            return (keys_hi, keys_lo)[k][:, h, bass.ds(t.pair * (2 * P), 2 * P)]
                    last = split_mm(ps_proj[:, half * 2 * P:(half + 1) * 2 * P],
                                    lambda k, h: w_q[:, k, h, half * P:(half + 1) * P], rows)
                last.then_inc(q_mm, 1)

            def edge_values(t):
                pe.wait_ge(q_lo, t.m + 1)
                for par in range(2):
                    last = split_mm(ps_proj[:, par * D:(par + 1) * D],
                                    lambda k, h: r_split[:, k, h, par * P:(par + 1) * P],
                                    lambda k, h: w_ev[:, k, h])
                last.then_inc(edge_mm, 1)

            def scores(t, c):
                dst = ps_scores[c % 2]
                for h in range(H):
                    for k, keys in ((0, keys_hi), (0, keys_lo), (1, keys_hi)):
                        for b in range(CHUNK // BANK):
                            col = c * CHUNK + b * BANK
                            last = nc.tensor.matmul(dst[:, b * BANK:(b + 1) * BANK],
                                                    q_split[:, k, h, t.par * P:(t.par + 1) * P],
                                                    keys[:, h, col:col + BANK],
                                                    start=h == 0 and k == 0 and keys is keys_hi,
                                                    stop=h == H - 1 and k == 1, skip_group_check=True)
                last.then_inc(scores_mm, 1)

            def prob_transposes(t, g):
                if g % 2 == 0:
                    pe.wait_ge(exped, t.n * CHUNKS + (g // 2 + 1))
                for b in range(GROUP):
                    col = (g * GROUP + b) * P
                    last = nc.tensor.transpose(ps_t[g % 2][:, b * P:(b + 1) * P], probs[:, t.par, col:col + P],
                                               ident[:])
                last.then_inc(pt_mm, 1)

            def values_product(t, g, dst):
                for b in range(GROUP):
                    j, sl = g * GROUP + b, slice(b * P, (b + 1) * P)
                    nc.tensor.matmul(dst[:], pt_hi[:, g % RING, sl], values[:, j, :],
                                     start=j == 0, stop=False, skip_group_check=True)
                    last = nc.tensor.matmul(dst[:, 0:D], pt_lo[:, g % RING, sl], values[:, j, 0:D],
                                            start=False, stop=j == TILES - 1, skip_group_check=True)
                last.then_inc(pv_mm, 1)

            def global_products():
                pe.wait_ge(mean_step, 1 + H)
                pe.wait_ge(biases_in, 16 * 5)
                for h in range(H):
                    for k in range(H):
                        last = nc.tensor.matmul(ps_proj[:, h * P:(h + 1) * P], wgk[:, k, h * P:(h + 1) * P],
                                                x_bar[:, k], start=k == 0, stop=k == H - 1)
                last.then_inc(global_mm, 1)
                for k in range(H):
                    last = nc.tensor.matmul(ps_out[:, 0:D], x_bar[:, k], wgv[:, k], start=k == 0, stop=k == H - 1)
                last.then_inc(global_mm, 1)

            def global_vector():
                pe.wait_ge(global_set, 1)
                for k in range(H):
                    last = nc.tensor.matmul(ps_t[0][:, 0:D], gk[:, k], wgq_t[:, k], start=k == 0, stop=k == H - 1)
                last.then_inc(global_mm, 1)

            def step(cur, nxt, far):
                for c in range(CHUNKS):
                    if cur is None and nxt.layer == 0 and c == 1:
                        global_products()
                    if cur is None and nxt.layer == 0 and c == 2:
                        global_vector()
                    if c == 3:
                        if far is not None and far.par == 0 and far.layer == 0:
                            pe.wait_ge(q_lo, far.m)
                            pe.wait_ge(edge_set, far.n)
                            query_transposes(far)
                        if cur is not None and nxt is not None:
                            prob_transposes(cur, 0)
                            prob_transposes(cur, 1)
                    if nxt is not None:
                        if c == 0:
                            pe.wait_ge(q_lo, nxt.m + 1)
                        if cur is None and c < 2:
                            pe.wait_ge(value_lo, UNITS * (nxt.layer + 1) - 2 + 2 * c)
                        else:
                            pe.wait_ge(masked, nxt.n * CHUNKS + (c - 1))
                        scores(nxt, c)
                if cur is None and nxt.layer == 0:
                    pe.wait_ge(global_set, 3)
                    edge_values(nxt)
                if cur is not None:
                    for g in range(GROUPS):
                        pe.wait_ge(pt_lo_set, cur.n * GROUPS + (g + 1))
                        if g + 2 < GROUPS:
                            prob_transposes(cur, g + 2)
                        elif far is None and nxt is not None:
                            prob_transposes(nxt, g + 2 - GROUPS)
                        elif nxt is None and cur.layer == 0 and g + 2 == GROUPS:
                            key_transposes(Unit(1, 0, 0))
                        if g == 0 and nxt is not None:
                            wait_used(pe, out_read, cur.n)
                        values_product(cur, g, ps_out if nxt is not None else ps_proj)
                        if g == 1 and far is not None and far.par == 0:
                            query_product(far)
                        if g == 3 and nxt is not None and nxt.par == 0 and nxt.layer == 0:
                            edge_values(nxt)

            def first_queries():
                pe.wait_ge(setup_lo, 4)
                query_product(Tile(0, 0, 0))
                pe.wait_ge(setup_lo, 6)
                pe.wait_ge(ones_set, 3)

            def layer_1_queries():
                pe.wait_ge(w_q1_in, 16)
                pe.wait_ge(out_read, TILES)
                pe.wait_ge(keys_hi_set, UNITS + 1)
                pe.wait_ge(keys_lo_set, UNITS + 1)
                query_product(Tile(1, 0, 0))

            pe.wait_ge(ident_set, 1)
            pe.wait_ge(weights_in[0], 16 * 2)
            transpose_w(ps_t[0], raw["Wlq"]).then_inc(setup_mm, 1)
            transpose_w(ps_t[1], raw["Wlk"]).then_inc(setup_mm, 1)
            pe.wait_ge(weights_in[1], 16 * 2)
            weight_product(ps_value[0], raw["Wq"], raw["Wk"]).then_inc(setup_mm, 1)
            pe.wait_ge(setup_lo, 2)
            weight_product(ps_value[2], wlq_t, wlk_t).then_inc(setup_mm, 1)
            query_transposes(Tile(0, 0, 0))
            pe.wait_ge(weights_in[2], 16 * 5)
            transpose_w(ps_out, raw["Wgq"]).then_inc(setup_mm, 1)
            transpose_w(ps_value[1], raw["Wv"]).then_inc(setup_mm, 1)

            key_transposes(Unit(0, 0, 0))
            first_queries()
            for layer in range(2):
                if layer:
                    pe.wait_ge(w_v1_in, 16)
                units(pe, layer, key_value_unit, layer_1_queries if layer else None)
                pe.wait_ge(keys_hi_set, UNITS * (layer + 1))
                pe.wait_ge(keys_lo_set, UNITS * (layer + 1))
                steps(pe, layer, step)

        @block.scalar
        def _(act):
            def hi(dst, src, **kw):
                return nc.scalar.activation(dst, src, ACT.Copy, **kw)

            def unit_values(v, k):
                return values[:, bass.ds(v.u * UNIT, UNIT), k * D:(k + 1) * D]

            def key_value_unit(t, v, w):
                if t is not None:
                    act.wait_ge(xt_mm, t.n + 1)
                    if t.layer or not isinstance(t.u, int) or t.u >= 2:
                        act.wait_ge(value_mm, t.n - 1)
                    hi(x_hi[:, t.slot], ps_t[t.slot][:]).then_inc(xt_hi, 1)
                if w is not None:
                    act.wait_ge(value_mm, w.n + 1)
                    hi(unit_values(w, 0), ps_value[w.b]).then_inc(value_hi, 1)
                if t is not None:
                    act.wait_ge(xt_hi, t.n + 1)
                    hi(keys_hi[:, :, bass.ds(t.u * (UNIT * P), UNIT * P)], f32(x_hi[:, t.slot])).then_inc(keys_hi_set, 1)

            def mask_chunk(t, c):
                if t.layer == 0:
                    if c == 0:
                        act.wait_ge(adj_in[t.par], t.layer_loads())
                    src = adj8[:, t.par * N + c * CHUNK:t.par * N + (c + 1) * CHUNK]
                else:
                    act.wait_ge(adj_t_in[c], t.layer_loads())
                    src = adj8[:].rearrange("p (j two) -> p two j", two=2)[:, t.par, c * CHUNK:(c + 1) * CHUNK]
                nc.scalar.activation(mask[:, c], src, ACT.Copy, scale=-MASKED[t.layer], bias=MASKED[t.layer]
                                     ).then_inc(mask_set, 1)

            def next_mask(t, c):
                act.wait_ge(masked, t.n * CHUNKS + (c + 1 - CHUNKS))
                mask_chunk(t, c)

            def exp_chunk(t, c):
                if c == 0:
                    act.wait_ge(max_set, t.n + 1)
                    wait_used(act, sums_used, t.n - 1)
                    if t.layer == 0:
                        nc.scalar.activation(ge_exp[:, t.par], row_max[:, t.par, 4:6], ACT.Exp,
                                             bias=neg_max[:, t.par:t.par + 1], accum_out=sums[:, t.par, 4:5])
                chunk = probs[:, t.par, c * CHUNK:(c + 1) * CHUNK]
                nc.scalar.activation(chunk, chunk, ACT.Exp, bias=neg_max[:, t.par:t.par + 1],
                                     accum_out=sums[:, t.par, c:c + 1]).then_inc(exped, 1)

            def query_rows_hi(t):
                act.wait_ge(rt_mm, t.m + 1)
                hi(r_split[:, 0], ps_proj[:]).then_inc(rt_hi, 1)

            def query_hi(t):
                act.wait_ge(q_mm, t.m + 1)
                hi(*query_halves(t, 0)).then_inc(q_hi, 1)

            def prob_hi(t, g):
                act.wait_ge(pt_mm, t.n * GROUPS + (g + 1))
                if g < RING:
                    last_group = max(k for k in range(GROUPS) if k % RING == g)
                    wait_used(act, pv_mm, t.n * GROUPS + (last_group + 1 - GROUPS))
                else:
                    act.wait_ge(pv_mm, t.n * GROUPS + (g + 1 - RING))
                hi(pt_hi[:, g % RING], ps_t[g % 2][:]).then_inc(pt_hi_set, 1)

            def step(cur, nxt, far):
                queries = far is not None and far.par == 0
                masks = far is not None
                if cur is not None and nxt is None:
                    prob_hi(cur, 0)
                    exp_chunk(cur, 2)
                    prob_hi(cur, 1)
                    exp_chunk(cur, 3)
                elif cur is not None:
                    exp_chunk(cur, 2)
                    exp_chunk(cur, 3)
                if masks:
                    next_mask(far, 0)
                    next_mask(far, 1)
                if queries and far.layer == 0:
                    query_rows_hi(far)
                if cur is not None and nxt is not None:
                    prob_hi(cur, 0)
                    prob_hi(cur, 1)
                if masks:
                    next_mask(far, 2)
                if cur is not None:
                    prob_hi(cur, 2)
                if masks:
                    next_mask(far, 3)
                if cur is not None:
                    prob_hi(cur, 3)
                if nxt is not None:
                    exp_chunk(nxt, 0)
                if queries:
                    query_hi(far)
                if cur is not None:
                    prob_hi(cur, 4)
                if nxt is not None:
                    exp_chunk(nxt, 1)
                if cur is not None and nxt is None and cur.layer == 0:
                    for c in range(CHUNKS):
                        next_mask(Tile(1, 0, 0), c)
                        if c < GROUPS - 5:
                            prob_hi(cur, c + 5)
                    key_value_unit(Unit(1, 0, 0), None, None)
                elif cur is not None:
                    for g in range(5, GROUPS):
                        prob_hi(cur, g)

            act.wait_ge(setup_mm, 3)
            hi(w_q1[:, 0], ps_value[0]).then_inc(setup_hi, 1)
            act.wait_ge(setup_mm, 4)
            hi(w_q[:, 0], ps_value[2], scale=SCALE).then_inc(setup_hi, 1)
            first = Tile(0, 0, 0)
            query_rows_hi(first)
            act.wait_ge(weights_in[2], 16 * 5)
            hi(w_v[:, 0], raw["Wlv"][:]).then_inc(setup_hi, 1)
            hi(blv_split[:], blv[:]).then_inc(setup_hi, 1)
            key_value_unit(Unit(0, 0, 0), None, None)
            query_hi(first)
            hi(w_ev[:, 0], raw["Wev"][:]).then_inc(setup_hi, 1)
            act.wait_ge(setup_mm, 5)
            hi(wgq_t[:], ps_out[:]).then_inc(setup_hi, 1)
            act.wait_ge(setup_mm, 6)
            hi(w_v1[:, 0], ps_value[1]).then_inc(setup_hi, 1)
            for layer in range(2):
                units(act, layer, key_value_unit, (lambda: query_hi(Tile(1, 0, 0))) if layer else None)
                if layer == 0:
                    for c in range(CHUNKS):
                        mask_chunk(first, c)
                steps(act, layer, step)

        @block.vector
        def _(dve):
            def lo(dst, src, hi_half):
                return nc.vector.tensor_tensor(dst, src, f32(hi_half), ALU.subtract)

            def unit_values(v, k):
                return values[:, bass.ds(v.u * UNIT, UNIT), k * D:(k + 1) * D]

            def key_value_unit(t, v, w):
                if t is not None:
                    dve.wait_ge(xt_hi, t.n + 1)
                    if t.layer == 0 and (not isinstance(t.u, int) or t.u >= 2):
                        dve.wait_ge(keys_lo_set, t.n - 1)
                    lo(x_lo[:, t.slot], ps_t[t.slot][:], x_hi[:, t.slot]).then_inc(xt_lo, 1)
                    if t.layer == 0:
                        nc.vector.tensor_reduce(x_sums[:, bass.ds(t.u, 1), :].rearrange("p o h -> p (o h)"),
                                                ps_t[t.slot][:].rearrange("p (h j) -> p h j", h=H),
                                                AX.X, ALU.add).then_inc(x_summed, 1)
                if w is not None:
                    dve.wait_ge(value_hi, w.n + 1)
                    lo(unit_values(w, 1), ps_value[w.b], unit_values(w, 0)).then_inc(value_lo, 1)
                if t is not None and t.layer == 1:
                    dve.wait_ge(xt_lo, t.n + 1)
                    nc.vector.tensor_copy(keys_lo[:, :, bass.ds(t.u * (UNIT * P), UNIT * P)], f32(x_lo[:, t.slot])
                                          ).then_inc(keys_lo_set, 1)

            def mean_row():
                dve.wait_ge(x_summed, UNITS)
                nc.vector.tensor_reduce(x_total[:], x_sums[:].rearrange("p j h -> p h j"), AX.X, ALU.add
                                        ).then_inc(mean_step, 1)
                dve.wait_ge(mean_step, 1)
                dve.wait_ge(ones_set, 1)
                for h in range(H):
                    nc.vector.tensor_scalar(x_bar[:, h], ones_f[:], x_total[:, h:h + 1], 1.0 / N, ALU.mult, ALU.mult
                                            ).then_inc(mean_step, 1)

            def global_key_value():
                dve.wait_ge(global_mm, 1)
                nc.vector.tensor_copy(gk[:], ps_proj[:, 0:D]).then_inc(global_set, 1)
                dve.wait_ge(biases_in, 16 * 5)
                dve.wait_ge(global_mm, 2)
                nc.vector.tensor_tensor(gv_bc[:], ps_out[:, 0:D], gv_bc[:], ALU.add).then_inc(global_set, 1)

            def global_vector():
                dve.wait_ge(global_mm, 3)
                nc.vector.tensor_scalar(u_bc[:], ps_t[0][:, 0:D], SCALE, None, ALU.mult).then_inc(global_set, 1)
                dve.wait_ge(global_set, 3)

            def row_dots(t):
                dve.wait_ge(rows_q_in, t.loads())
                wait_used(dve, exped, t.n * CHUNKS + (1 - 2 * CHUNKS))
                for k, vec, dot in ((0, u_bc, global_dot), (1, wes_bc, edge_dot)):
                    nc.vector.tensor_tensor_reduce(out=dot_out[:], in0=rows_q[:, t.par], in1=vec[:], scale=1.0,
                                                   scalar=0.0, op0=ALU.mult, op1=ALU.add,
                                                   accum_out=row_max[:, t.par, 4 + k:5 + k]).then_inc(dot, 1)
                    dve.wait_ge(dot, t.n + 1)

            def query_rows_lo(t):
                dve.wait_ge(rt_hi, t.m + 1)
                lo(r_split[:, 1], ps_proj[:], r_split[:, 0]).then_inc(rt_lo, 1)

            def query_lo(t):
                dve.wait_ge(q_hi, t.m + 1)
                lo(*query_halves(t, 1), query_halves(t, 0)[0]).then_inc(q_lo, 1)

            def edge_rows(t):
                dve.wait_ge(edge_mm, t.m + 1)
                nc.vector.tensor_tensor(edge_v[:, t.par], ps_proj[:, t.par * D:(t.par + 1) * D], bev_bc[:], ALU.add
                                        ).then_inc(edge_set, 1)

            def mask_scores(t, c):
                count = dve.compute_val(t.n * CHUNKS + (c + 1))
                dve.wait_ge(keys_lo_set, UNITS * (t.layer + 1))
                dve.wait_ge(mask_set, count)
                dve.wait_ge(scores_mm, count)
                nc.vector.tensor_tensor_reduce(out=probs[:, t.par, c * CHUNK:(c + 1) * CHUNK], in0=ps_scores[c % 2][:],
                                               in1=mask[:, c], scale=1.0, scalar=-3e38, op0=ALU.add, op1=ALU.max,
                                               accum_out=row_max[:, t.par, c:c + 1]).then_inc(masked, 1)

            def set_max(t):
                dve.wait_ge(masked, t.n * CHUNKS + CHUNKS)
                wait_used(dve, exped, t.n * CHUNKS - CHUNKS)
                nc.vector.tensor_reduce(neg_max[:, t.par:t.par + 1], row_max[:, t.par, 0:6 if t.layer == 0 else 5],
                                        AX.X, ALU.max, negate=True).then_inc(max_set, 1)

            def prob_lo(t, g):
                dve.wait_ge(pt_hi_set, t.n * GROUPS + (g + 1))
                lo(pt_lo[:, g % RING], ps_t[g % 2][:], pt_hi[:, g % RING]).then_inc(pt_lo_set, 1)

            def epi_then(t, k, ins):
                before = t.n * EPI_STEPS[t.layer] + TILES * (t.layer * (EPI_STEPS[0] - EPI_STEPS[1]))
                ins.then_inc(epi_step, 1)
                dve.wait_ge(epi_step, before + k)

            def row_weights(t):
                p = t.par
                d, r = den[:, p:p + 1], rden[:, 0:1]
                dve.wait_ge(exped, t.n * CHUNKS + CHUNKS)
                if t.layer == 0:
                    epi_then(t, 1, nc.vector.reduce_sum(d, sums[:, p, 0:5], AX.X))
                    epi_then(t, 2, nc.vector.reciprocal(r, d))
                    nc.vector.tensor_scalar(ge_w[:], ge_exp[:, p], r, None, ALU.mult).then_inc(sums_used, 1)
                    dve.wait_ge(sums_used, t.n + 1)
                    epi_then(t, 3, nc.vector.tensor_scalar(y_tmp[:], gv_bc[:], ge_w[:, 0:1], None, ALU.mult))
                    dve.wait_ge(edge_set, t.n + 1)
                    epi_then(t, 4, nc.vector.scalar_tensor_tensor(
                        out=y_tmp[:], in0=edge_v[:, p], scalar=ge_w[:, 1:2], in1=y_tmp[:], op0=ALU.mult, op1=ALU.add))
                else:
                    nc.vector.reduce_sum(d, sums[:, p, 0:4], AX.X).then_inc(sums_used, 1)
                    dve.wait_ge(sums_used, t.n + 1)
                    epi_then(t, 1, nc.vector.tensor_scalar(d, d, TINY, None, ALU.max))
                    epi_then(t, 2, nc.vector.reciprocal(r, d))

            def add_product(t, product):
                p, r = t.par, rden[:, 0:1]
                if t.layer == 0:
                    add, out_t, k = y_tmp[:], y_tmp[:], 5
                    dve.wait_ge(rows_res_in[0][p], t.layer_loads(2))
                else:
                    add, out_t, k = rows_max[:, p], rows_res[:, p], 3
                    dve.wait_ge(rows_res_in[1][p], t.layer_loads())
                    dve.wait_ge(normed, t.n - 1)
                dve.wait_ge(pv_mm, t.n * GROUPS + GROUPS)
                epi_then(t, k, nc.vector.scalar_tensor_tensor(out=y_tmp[:], in0=product[:, 0:D], scalar=r, in1=add,
                                                              op0=ALU.mult, op1=ALU.add))
                nc.vector.scalar_tensor_tensor(out=out_t, in0=product[:, D:2 * D], scalar=r, in1=y_tmp[:],
                                               op0=ALU.mult, op1=ALU.add).then_inc(out_read, 1)
                dve.wait_ge(out_read, t.n + 1)

            def row_stats(t):
                p = t.par
                if t.layer == 0:
                    epi_then(t, 6, nc.vector.tensor_tensor(y_tmp[:], y_tmp[:], rows_max[:, p], ALU.max))
                    epi_then(t, 7, nc.vector.tensor_tensor(rows_res[:, p], y_tmp[:], rows_res[:, p], ALU.add))
                nc.vector.bn_stats(stats[:], rows_res[:, p])
                dve.drain()
                nc.vector.bn_aggr(mean_var[:, p], stats[:]).then_inc(stats_set, 1)

            def step(cur, nxt, far):
                queries = far is not None and far.par == 0
                edges = nxt is not None and nxt.par == 0 and nxt.layer == 0
                if cur is None and edges:
                    mask_scores(nxt, 0)
                    global_key_value()
                    mask_scores(nxt, 1)
                    global_vector()
                    row_dots(nxt)
                    mask_scores(nxt, 2)
                elif nxt is not None:
                    mask_scores(nxt, 0)
                    mask_scores(nxt, 1)
                    mask_scores(nxt, 2)
                if queries and far.layer == 0:
                    query_rows_lo(far)
                if cur is not None and nxt is not None:
                    prob_lo(cur, 0)
                    prob_lo(cur, 1)
                if nxt is not None:
                    mask_scores(nxt, 3)
                    set_max(nxt)
                if cur is None and edges:
                    row_dots(far)
                    edge_rows(nxt)
                    edge_rows(nxt.after(1))
                if cur is not None:
                    for g in range(2, GROUPS):
                        prob_lo(cur, g)
                        if g == 3 and queries:
                            query_lo(far)
                        if g == 4 and far is not None and far.layer == 0:
                            row_dots(far)
                        if g == 5 and edges:
                            edge_rows(nxt)
                        if nxt is None and g == 2:
                            last = Tile(cur.layer, cur.pair, 0)
                            add_product(last, ps_out)
                        if nxt is None and g == 3:
                            row_stats(last)
                        if g == 6:
                            row_weights(cur)
                    if nxt is None and cur.layer == 0:
                        key_value_unit(Unit(1, 0, 0), None, None)
                    if far is None and nxt is not None:
                        prob_lo(nxt, 0)
                        prob_lo(nxt, 1)
                    else:
                        add_product(cur, ps_out if nxt is not None else ps_proj)
                        row_stats(cur)
                    if edges:
                        edge_rows(nxt.after(1))

            dve.wait_ge(setup_mm, 1)
            nc.vector.tensor_copy(wlq_t[:], ps_t[0][:]).then_inc(setup_lo, 1)
            dve.wait_ge(setup_mm, 2)
            nc.vector.tensor_copy(wlk_t[:], ps_t[1][:]).then_inc(setup_lo, 1)
            dve.wait_ge(setup_hi, 1)
            lo(w_q1[:, 1], ps_value[0], w_q1[:, 0]).then_inc(setup_lo, 1)
            dve.wait_ge(setup_hi, 2)
            nc.vector.scalar_tensor_tensor(out=w_q[:, 1], in0=ps_value[2], scalar=SCALE,
                                           in1=f32(w_q[:, 0]), op0=ALU.mult, op1=ALU.subtract).then_inc(setup_lo, 1)
            first = Tile(0, 0, 0)
            query_rows_lo(first)
            dve.wait_ge(setup_hi, 4)
            lo(w_v[:, 1], raw["Wlv"][:], w_v[:, 0]).then_inc(setup_lo, 1)
            row = slice(BIAS_ROWS - 1, BIAS_ROWS)
            lo(blv_split[row], blv[row], blv_split[row]).then_inc(setup_lo, 1)
            key_value_unit(Unit(0, 0, 0), None, None)
            query_lo(first)
            dve.wait_ge(setup_hi, 5)
            lo(w_ev[:, 1], raw["Wev"][:], w_ev[:, 0]).then_inc(setup_lo, 1)
            dve.wait_ge(setup_hi, 7)
            lo(w_v1[:, 1], ps_value[1], w_v1[:, 0]).then_inc(setup_lo, 1)
            for layer in range(2):
                units(dve, layer, key_value_unit, (lambda: query_lo(Tile(1, 0, 0))) if layer else None)
                if layer == 0:
                    mean_row()
                    dve.wait_ge(w1_out, 32)
                else:
                    for par in range(2):
                        nc.vector.memset(row_max[:, par, 4:5], FLOOR).then_inc(floor_set, 1)
                    dve.wait_ge(floor_set, 2)
                steps(dve, layer, step)


_INS = ['x', 'adj', 'L0_gnn_masked_x', 'L0_gnn_Wlq', 'L0_gnn_Wlk', 'L0_gnn_Wlv', 'L0_gnn_blv', 'L0_gnn_Wgq',
        'L0_gnn_Wgk', 'L0_gnn_Wgv', 'L0_gnn_bgv', 'L0_gnn_Wes', 'L0_gnn_Wev', 'L0_gnn_bev', 'L1_gnn_Wq',
        'L1_gnn_Wk', 'L1_gnn_Wv']


def kernel(**inputs):
    import numpy as _np
    import concourse.bacc as _bacc
    from concourse import mybir as _mybir
    from concourse.bass_utils import run_bass_kernel_spmd as _run

    nc = _bacc.Bacc("TRN2", target_bir_lowering=False, num_devices=1, dynamic_dma_scratch_size=1024)
    arrays, args = {}, {}
    for name in _INS:
        arr = _np.ascontiguousarray(inputs[name])
        arrays[f"in_{name}_dram"] = arr
        args[name] = nc.dram_tensor(f"in_{name}_dram", arr.shape, _mybir.dt.from_np(arr.dtype),
                                    kind="ExternalInput").ap()
    out = nc.dram_tensor("out_dram", (N, D), _mybir.dt.float32, kind="ExternalOutput").ap()
    adj_resnorm(nc, args, out)
    r = _run(nc, [arrays], core_ids=[0])
    return r.results[0]["out_dram"]
```
